# Optimizing a Trainium2 kernel written in Bass

```python
import numpy as np
import jax
import jax.numpy as jnp

def _softmax(x, axis=-1):
    return jax.nn.softmax(x, axis=axis)
def _gelu(x):
    return jax.nn.gelu(x, approximate=True)
def _silu(x):
    return jax.nn.silu(x)
def _sigmoid(x):
    return jax.nn.sigmoid(x)
def _layernorm(x, axis=-1, eps=1e-5):
    m = jnp.mean(x, axis=axis, keepdims=True)
    v = jnp.var(x, axis=axis, keepdims=True)
    return (x - m) / jnp.sqrt(v + eps)
def _scatter_add(tgt, idx, src, axis=0):
    return tgt.at[idx].add(src)
def _segment_sum(src, seg, n):
    return jax.ops.segment_sum(src, seg, n)

kernel_name = 'mk_conv_preact_d1_conv_nchw128_846b3b'

def setup_inputs(seed: int = 0):
    np.random.seed(seed)
    _w = jnp.asarray
    def _rec_inputs():
        import jax
        import jax.numpy as jnp
        _gk = jax.random.key(seed)
        x = -0.0001142 + 0.9999 * jax.random.normal(jax.random.fold_in(_gk, 1), (64, 128, 36, 100), jnp.float32)
        return x
    x = _rec_inputs()
    def _L0_conv_setup():
        import jax, jax.numpy as jnp
        import numpy as np
        B, C, H, W = (64, 128, 36, 100)
        KSZ = 9
        PAD = 4
        key = jax.random.key(seed)
        k1, k2 = jax.random.split(key, 2)
        x = jax.random.normal(k1, (B, C, H, W), dtype=jnp.float32)
        kernel = jax.random.normal(k2, (C, KSZ, 1, C), dtype=jnp.float32) * 0.02
        bias = jnp.zeros((C,), dtype=jnp.float32)
        return {'x': x, 'kernel': kernel, 'bias': bias}
    _L0_conv_all = _L0_conv_setup()
    _L0_conv_in = {k: v for k, v in _L0_conv_all.items() if k in ('kernel', 'bias', )}
    del _L0_conv_all

    return {
        "x": x,
        "L0_conv_kernel": _L0_conv_in["kernel"],
        "L0_conv_bias": _L0_conv_in["bias"],
    }

def reference(x, L0_conv_kernel, L0_conv_bias):
    import jax
    import jax.numpy as jnp
    def _L0_conv_ref(x, kernel, bias):
        import jax, jax.numpy as jnp
        import numpy as np
        B, C, H, W = (64, 128, 36, 100)
        KSZ = 9
        PAD = 4
        w = jnp.transpose(kernel[:, :, 0, :], (2, 0, 1))

        def conv_row(row):
            return jax.lax.conv_general_dilated(row, w, window_strides=(1,), padding=[(PAD, PAD)], dimension_numbers=('NCH', 'OIH', 'NCH'))

        def step(carry, x_row):
            inp = x_row + carry
            out = jax.nn.relu(conv_row(inp) + bias[None, :, None])
            return (out, out)
        x_rows = jnp.transpose(x, (2, 0, 1, 3))
        _, outs = jax.lax.scan(step, jnp.zeros_like(x_rows[0]), x_rows)
        return jnp.transpose(outs, (1, 2, 0, 3))

    def _gn(v, G=32, eps=1e-5):
        B_, C_, H_, W_ = v.shape
        g = v.reshape(B_, G, C_ // G, H_, W_)
        m = jnp.mean(g, axis=(2, 3, 4), keepdims=True)
        s = jnp.var(g, axis=(2, 3, 4), keepdims=True)
        return ((g - m) / jnp.sqrt(s + eps)).reshape(v.shape)

    def _ln_c(v, eps=1e-6):
        m = jnp.mean(v, axis=1, keepdims=True)
        s = jnp.var(v, axis=1, keepdims=True)
        return (v - m) / jnp.sqrt(s + eps)

    def _ln_t(v, eps=1e-5):
        m = jnp.mean(v, axis=-1, keepdims=True)
        s = jnp.var(v, axis=-1, keepdims=True)
        return (v - m) / jnp.sqrt(s + eps)

    def _to_tokens(v):
        B_, C_, H_, W_ = v.shape
        return v.reshape(B_, C_, H_ * W_).transpose(0, 2, 1)
    def _from_tokens(t, like):
        B_, C_, H_, W_ = like.shape
        return t.transpose(0, 2, 1).reshape(B_, C_, H_, W_)

    x = x + _L0_conv_ref(_gn(x), L0_conv_kernel, L0_conv_bias)
    return x


_drawn_inputs = setup_inputs


def setup_inputs(seed=0):
    import zlib

    import numpy as np

    out = dict(_drawn_inputs(seed))
    spreads = {'L0_conv_bias': (0.0, 0.1)}
    factors = {}
    for name, (base, spread) in spreads.items():
        noise = np.random.default_rng([zlib.crc32(name.encode()), seed]).standard_normal(out[name].shape)
        drawn = base * np.exp(spread * noise) if base else spread * noise
        out[name] = jnp.asarray(drawn.astype(out[name].dtype))
    for name, factor in factors.items():
        out[name] = (out[name] * factor).astype(out[name].dtype)
    return out
```

```python
import concourse.bass as bass
from concourse import mybir
from contextlib import ExitStack


def conv_scan_kernel(nc: bass.Bass, x: bass.AP, taps: bass.AP, bias: bass.AP, out: bass.AP):
    f32 = mybir.dt.float32
    f32r = mybir.dt.float32r
    ALU = mybir.AluOpType
    ACT = mybir.ActivationFunctionType

    IMAGES, C, H, W = x.shape
    TAPS = taps.shape[1]
    PAD = TAPS // 2
    NORM_GROUP = 4
    EPS = 1e-5

    G = 5
    GROUPS = -(-IMAGES // G)
    HALF = H // 2
    CHUNK = HALF // 2
    STATS_ROWS = (3, 3 + G)
    COLS = G * W
    U = W // 2
    PAIRS = TAPS // 2
    Q = W + 2 * PAD
    V = Q // 2
    YOUNG_SLOTS, OLD_SLOTS = 3, 5
    BN = CHUNK * W // 2
    BN_PER_IMAGE = 4 * 2
    EVEN_W, ODD_W, SUM_W, LAST_W = 0, PAIRS, 2 * PAIRS, 3 * PAIRS
    WEIGHTS = 3 * PAIRS + 1
    CHAINS = ("young", "old")

    x_view = x.rearrange("b c h w -> c b (h w)")
    out_view = out.rearrange("b c h w -> c b (h w)")

    def first_image(g):
        return 0 if isinstance(g, int) and g == 0 else g * G - (G * GROUPS - IMAGES)

    ctx = ExitStack()
    with ctx:
        def sb(name, shape, dt=f32):
            return ctx.enter_context(nc.sbuf_tensor(name, shape, dt))

        def sem(name):
            return ctx.enter_context(nc.semaphore(name))

        def pair_of(make, name):
            return {c: make(f"{name}_{c}") for c in CHAINS}

        x_young = sb("x_young", [C, YOUNG_SLOTS, G, CHUNK * W])
        x_old = sb("x_old", [C, OLD_SLOTS, G, CHUNK * W])
        x_ring = {"young": (x_young, YOUNG_SLOTS), "old": (x_old, OLD_SLOTS)}

        w_high = sb("w_high", [C, WEIGHTS, C], f32r)
        w_low = sb("w_low", [C, WEIGHTS, C], f32r)
        bias_col = sb("bias_col", [C, 1])

        y = pair_of(lambda n: sb(n, [C, COLS]), "y")
        shared = pair_of(lambda n: sb(n, [C, G * U]), "shared")
        x_norm = pair_of(lambda n: sb(n, [C, COLS]), "x_norm")
        q_row = sb("q_row", [C, G, Q])
        d_row = sb("d_row", [C, G, Q])
        q_high = pair_of(lambda n: sb(n, [C, 2, G, V], f32r), "q_high")
        q_low = pair_of(lambda n: sb(n, [C, 2, G, V], f32r), "q_low")
        d_high = pair_of(lambda n: sb(n, [C, 2, G, V], f32r), "d_high")
        d_low = pair_of(lambda n: sb(n, [C, 2, G, V], f32r), "d_low")

        group_mean = sb("group_mean", [C, C])
        bn = sb("bn", [C, G, BN_PER_IMAGE * 6])
        mean_var = sb("mean_var", [C, G, 2])
        stat = sb("stat", [C, 6, G])
        norm = pair_of(lambda n: sb(n, [C, 2, G]), "norm")

        y_ps = pair_of(lambda n: ctx.enter_context(nc.psum_tensor(n, [C, 512], f32)), "y_ps")
        sum_ps = pair_of(lambda n: ctx.enter_context(nc.psum_tensor(n, [C, 512], f32)), "sum_ps")
        stat_ps = ctx.enter_context(nc.psum_tensor("stat_ps", [C, 2, G], f32))

        spare = x_young[:, YOUNG_SLOTS - 1, :, :].rearrange("p g n -> p (g n)")
        w_raw = spare[:, 0:TAPS * C].rearrange("p (k o) -> p k o", k=TAPS)
        w_sum = spare[:, TAPS * C:(TAPS + PAIRS) * C].rearrange("p (k o) -> p k o", k=PAIRS)

        weights_loaded = sem("weights_loaded")
        first_loaded = [sem(f"first_loaded{n}") for n in range(4)]
        chunk_loaded = pair_of(sem, "chunk_loaded")
        chunk_stored = pair_of(sem, "chunk_stored")
        mask_cleared = sem("mask_cleared")
        mask_ready = sem("mask_ready")
        pads_cleared = sem("pads_cleared")
        sums_made = sem("sums_made")
        high_made = sem("high_made")
        weights_ready = sem("weights_ready")
        sum_done = pair_of(sem, "sum_done")
        y_done = pair_of(sem, "y_done")
        shared_ready = pair_of(sem, "shared_ready")
        norm_ready = pair_of(sem, "norm_ready")
        y_ready = pair_of(sem, "y_ready")
        q_ready = pair_of(sem, "q_ready")
        d_ready = pair_of(sem, "d_ready")
        q_high_ready = pair_of(sem, "q_high_ready")
        d_high_ready = pair_of(sem, "d_high_ready")
        q_low_ready = pair_of(sem, "q_low_ready")
        d_low_ready = pair_of(sem, "d_low_ready")
        row_final = pair_of(sem, "row_final")
        bn_taken = sem("bn_taken")
        stats_step = sem("stats_step")
        newton = sem("newton")
        mean_in = sem("mean_in")
        mean_out = sem("mean_out")
        var_in = sem("var_in")
        var_out = sem("var_out")
        var_eps = sem("var_eps")
        root_ready = sem("root_ready")
        scales_ready = sem("scales_ready")

        block = ctx.enter_context(nc.Block())

        def chunk_of(chain, phase):
            ring, slots = x_ring[chain]
            return (phase if chain == "young" else phase - 2) % slots

        def x_row(chain, slot, r):
            ring, _ = x_ring[chain]
            return ring[:, bass.ds(slot, 1), :, bass.ds(r * W, W)].rearrange("p s g w -> p (s g) w")

        def by_image(a):
            return a[:, :].rearrange("p (g w) -> p g w", g=G)

        def parities(row, s, n):
            return row[:, :, s:s + n].rearrange("p g (v two) -> p two g v", two=2)

        STAT_STEPS = 6

        @block.sync
        def _(sp):
            sp.dma_start(w_raw, taps.rearrange("c k one o -> c k (one o)")).then_inc(weights_loaded, 16)
            sp.dma_start(bias_col[:, :], bias.rearrange("(c one) -> c one", one=1)).then_inc(weights_loaded, 16)

            def load(chain, phase, group, k, done):
                ring, slots = x_ring[chain]
                row = k * CHUNK + (HALF if chain == "old" else 0)
                sp.dma_start(
                    ring[:, bass.ds(phase % slots, 1), :, :].rearrange("p s g n -> p (s g) n"),
                    x_view[:, bass.ds(first_image(group), G), row * W:(row + CHUNK) * W],
                ).then_inc(done, 16)

            for k in range(2):
                load("young", k, 0, k, first_loaded[2 * k])
                load("old", k, 0, k, first_loaded[2 * k + 1])

            def store(chain, phase, group, k):
                ring, slots = x_ring[chain]
                row = k * CHUNK + (HALF if chain == "old" else 0)
                sp.dma_start(
                    out_view[:, bass.ds(first_image(group), G), row * W:(row + CHUNK) * W],
                    ring[:, bass.ds(chunk_of(chain, phase), 1), :, :].rearrange("p s g n -> p (s g) n"),
                ).then_inc(chunk_stored[chain], 16)

            def period(i, young, old, ahead):
                for k in range(2):
                    p = 2 * i + k
                    if ahead:
                        if isinstance(i, int) and p == 0:
                            sp.wait_ge(weights_ready, 1)
                        else:
                            sp.wait_ge(chunk_stored["young"], 16 * p)
                        if not isinstance(i, int) or p > 2:
                            sp.wait_ge(chunk_stored["old"], 16 * (p - 2))
                        load("young", p + 2, i + 1, k, chunk_loaded["young"])
                        load("old", p + 2, i + 1, k, chunk_loaded["old"])
                    if young:
                        sp.wait_ge(row_final["young"], HALF * i + CHUNK * (k + 1))
                        store("young", p, i, k)
                    if old:
                        sp.wait_ge(row_final["old"], HALF * (i - 1) + CHUNK * (k + 1))
                        store("old", p, i - 1, k)

            period(0, True, False, True)
            period(1, True, True, True)
            with sp.Fori(2, GROUPS - 1) as i:
                period(i, True, True, True)
            period(GROUPS - 1, True, True, False)
            period(GROUPS, False, True, False)
            sp.wait_ge(chunk_stored["young"], 16 * 2 * GROUPS)
            sp.wait_ge(chunk_stored["old"], 16 * 2 * GROUPS)

        @block.gpsimd
        def _(pool):
            nc.gpsimd.memset(group_mean[:, :], 1.0 / NORM_GROUP).then_inc(mask_cleared, 1)
            blocks = group_mean[:, :].rearrange("p (a b) -> p a b", b=NORM_GROUP)
            pool.wait_ge(mask_cleared, 1)
            nc.gpsimd.affine_select(out=blocks, in_=blocks, compare_op=ALU.is_ge, fill=0.0, base=0,
                                    pattern=[[-NORM_GROUP, C // NORM_GROUP], [0, NORM_GROUP]],
                                    channel_multiplier=1).then_inc(mask_cleared, 1)
            pool.wait_ge(mask_cleared, 2)
            nc.gpsimd.affine_select(out=blocks, in_=blocks, compare_op=ALU.is_ge, fill=0.0,
                                    base=NORM_GROUP - 1,
                                    pattern=[[NORM_GROUP, C // NORM_GROUP], [0, NORM_GROUP]],
                                    channel_multiplier=-1).then_inc(mask_ready, 1)

        @block.tensor
        def _(pe):
            def products(bank, weight, moving, start=False, stop=False):
                return nc.tensor.matmul(bank, weight, moving, start=start, stop=stop,
                                        skip_group_check=True)

            def row(c, n):
                even, odd = y_ps[c][:, 0:G * U], y_ps[c][:, G * U:COLS]
                both, total = y_ps[c][:, 0:COLS], sum_ps[c][:, 0:G * U]

                def shared_sum(w, moving, start=False, stop=False):
                    for j in range(PAIRS):
                        last = products(total, w[:, SUM_W + j, :], moving[:, 1, :, j:j + U],
                                        start and j == 0, stop and j == PAIRS - 1)
                    return last

                def last_tap(w, moving, start=False):
                    products(both, w[:, LAST_W, :], moving[:, :, :, PAIRS:PAIRS + U], start)

                def differences(w, moving, stop=False):
                    for j in range(PAIRS):
                        products(even, w[:, EVEN_W + j, :], moving[:, 0, :, j:j + U])
                        last = products(odd, w[:, ODD_W + j, :], moving[:, 1, :, j:j + U],
                                        stop=stop and j == PAIRS - 1)
                    return last

                pe.wait_ge(q_high_ready[c], n)
                shared_sum(w_high, q_high[c], start=True)
                last_tap(w_high, q_high[c], start=True)
                shared_sum(w_low, q_high[c])
                last_tap(w_low, q_high[c])
                pe.wait_ge(q_low_ready[c], n)
                shared_sum(w_high, q_low[c], stop=True).then_inc(sum_done[c], 1)
                last_tap(w_high, q_low[c])
                pe.wait_ge(d_high_ready[c], n)
                differences(w_high, d_high[c])
                differences(w_low, d_high[c])
                pe.wait_ge(d_low_ready[c], n)
                differences(w_high, d_low[c], stop=True).then_inc(y_done[c], 1)

            def average_means(g):
                pe.wait_ge(mean_in, g)
                nc.tensor.matmul(stat_ps[:, 0, :], group_mean[:, :], stat[:, 0, :],
                                 start=True, stop=True).then_inc(mean_out, 1)

            def average_variances(g):
                pe.wait_ge(var_in, g)
                nc.tensor.matmul(stat_ps[:, 1, :], group_mean[:, :], stat[:, 1, :],
                                 start=True, stop=True).then_inc(var_out, 1)

            pe.wait_ge(mask_ready, 1)
            average_means(1)
            average_variances(1)
            pe.wait_ge(weights_ready, 1)

            def period(i, young, old, ahead):
                for k in range(2):
                    with pe.Fori(0, CHUNK - 1) as r:
                        plain(i, k, r, young, old)
                    if k == 1 and ahead:
                        average_means(i + 2)
                        if young:
                            row("young", HALF * i + HALF)
                        average_variances(i + 2)
                        if old:
                            row("old", HALF * (i - 1) + HALF)
                    else:
                        plain(i, k, CHUNK - 1, young, old)

            def plain(i, k, r, young, old):
                if young:
                    row("young", HALF * i + CHUNK * k + r + 1)
                if old:
                    row("old", HALF * (i - 1) + CHUNK * k + r + 1)

            period(0, True, False, True)
            with pe.Fori(1, GROUPS - 1) as i:
                period(i, True, True, True)
            period(GROUPS - 1, True, True, False)
            period(GROUPS, False, True, False)

        @block.scalar
        def _(act):
            def normalise(c, slot, r):
                row = x_row(c, slot, r)
                for b in range(G):
                    last = nc.scalar.activation(by_image(x_norm[c])[:, b, :], row[:, b, :], ACT.Identity,
                                                scale=norm[c][:, 0, b:b + 1], bias=norm[c][:, 1, b:b + 1])
                last.then_inc(norm_ready[c], 1)

            def high_parts(c, n):
                act.wait_ge(q_ready[c], n)
                nc.scalar.activation(q_high[c][:, :, :, PAIRS // 2:PAIRS // 2 + U],
                                     parities(q_row, PAD, W), ACT.Copy).then_inc(q_high_ready[c], 1)
                act.wait_ge(d_ready[c], n)
                nc.scalar.activation(d_high[c][:, :, :, PAIRS // 2 - 1:PAIRS // 2 + U],
                                     parities(d_row, PAD - 2, W + 2), ACT.Copy).then_inc(d_high_ready[c], 1)

            def share(c, n):
                act.wait_ge(sum_done[c], n)
                nc.scalar.activation(shared[c][:, :], sum_ps[c][:, 0:G * U], ACT.Identity,
                                     bias=bias_col[:, 0:1]).then_inc(shared_ready[c], 1)

            def roots(g):
                act.wait_ge(var_eps, g)
                nc.scalar.activation(stat[:, 3, :], stat[:, 2, :], ACT.Sqrt).then_inc(root_ready, 1)

            roots(1)
            act.wait_ge(weights_loaded, 32)
            act.wait_ge(scales_ready, 1)
            act.wait_ge(pads_cleared, 1)
            normalise("young", 0, 0)
            high_parts("young", 1)

            def period(i, young, old, ahead):
                for k in range(2):
                    p = 2 * i + k
                    ny, no = HALF * i + CHUNK * k + 1, HALF * (i - 1) + CHUNK * k + 1
                    with act.Fori(0, CHUNK - 1) as r:
                        if young:
                            share("young", ny + r)
                            normalise("young", chunk_of("young", p), r + 1)
                            high_parts("young", ny + r + 1)
                        if old:
                            share("old", no + r)
                            normalise("old", chunk_of("old", p), r + 1)
                            high_parts("old", no + r + 1)
                    ny, no = ny + CHUNK - 1, no + CHUNK - 1
                    if young:
                        share("young", ny)
                        if k == 0:
                            normalise("young", chunk_of("young", p + 1), 0)
                            high_parts("young", ny + 1)
                        elif ahead:
                            roots(i + 2)
                            act.wait_ge(scales_ready, i + 2)
                            normalise("young", chunk_of("young", p + 1), 0)
                            high_parts("young", ny + 1)
                        else:
                            act.wait_ge(scales_ready, i + 2)
                    if old:
                        share("old", no)
                    if (k == 0 and old) or (k == 1 and young):
                        normalise("old", chunk_of("old", p + 1), 0)
                        high_parts("old", no + 1)

            period(0, True, False, True)
            with act.Fori(1, GROUPS - 1) as i:
                period(i, True, True, True)
            period(GROUPS - 1, True, True, False)
            period(GROUPS, False, True, False)

        @block.vector
        def _(dve):
            def clear(a):
                return nc.vector.memset(a, 0.0)

            for c in CHAINS:
                for a in (q_high[c], q_low[c], d_high[c], d_low[c]):
                    clear(a[:, :, :, :].bitcast(f32))
            clear(q_row[:, :, :]).then_inc(pads_cleared, 1)

            dve.wait_ge(weights_loaded, 32)
            pair = w_raw[:, 0:2 * PAIRS, :].rearrange("p (j two) o -> p two j o", two=2)
            nc.vector.tensor_tensor(w_sum, pair[:, 0, :, :], pair[:, 1, :, :], ALU.add).then_inc(sums_made, 1)
            nc.vector.tensor_copy(w_high[:, EVEN_W:EVEN_W + PAIRS, :], pair[:, 0, :, :])
            nc.vector.tensor_scalar(w_high[:, ODD_W:ODD_W + PAIRS, :], pair[:, 1, :, :], -1.0, None, ALU.mult)
            dve.wait_ge(sums_made, 1)
            nc.vector.tensor_copy(w_high[:, SUM_W:SUM_W + PAIRS, :], w_sum)
            nc.vector.tensor_copy(w_high[:, LAST_W, :], w_raw[:, TAPS - 1, :]).then_inc(high_made, 1)
            dve.wait_ge(high_made, 1)

            def low(at, n, full):
                return nc.vector.tensor_tensor(w_low[:, at:at + n, :], full,
                                               w_high[:, at:at + n, :].bitcast(f32), ALU.subtract)

            low(EVEN_W, PAIRS, pair[:, 0, :, :])
            for j in range(PAIRS):
                nc.vector.scalar_tensor_tensor(w_low[:, ODD_W + j, :], pair[:, 1, j, :], -1.0,
                                               w_high[:, ODD_W + j, :].bitcast(f32), ALU.mult, ALU.subtract)
            low(SUM_W, PAIRS, w_sum)
            low(LAST_W, 1, w_raw[:, TAPS - 1:TAPS, :]).then_inc(weights_ready, 1)

            def bn_chunk(chain, slot, k, b):
                ring, _ = x_ring[chain]
                for half in range(2):
                    at = 6 * (4 * k + 2 * (chain == "old") + half)
                    last = nc.vector.bn_stats(
                        bn[:, bass.ds(b, 1), at:at + 6].rearrange("p b s -> p (b s)"),
                        ring[:, bass.ds(slot, 1), bass.ds(b, 1), half * BN:half * BN + BN]
                        .rearrange("p s b n -> p (s b n)"))
                return last

            def channel_stats(g):
                for b in range(G):
                    last = nc.vector.bn_aggr(mean_var[:, b, :], bn[:, b, :])
                base = STAT_STEPS * (g - 1)
                last.then_inc(stats_step, 1)
                dve.wait_ge(stats_step, base + 1)
                nc.vector.tensor_copy(stat[:, 0, :], mean_var[:, :, 0]).then_inc(mean_in, 1)

            def group_variance(g):
                base = STAT_STEPS * (g - 1)
                dve.wait_ge(mean_out, g)
                nc.vector.tensor_tensor(stat[:, 4, :], mean_var[:, :, 0], stat_ps[:, 0, :],
                                        ALU.subtract).then_inc(stats_step, 1)
                dve.wait_ge(stats_step, base + 2)
                nc.vector.tensor_tensor(stat[:, 5, :], stat[:, 4, :], stat[:, 4, :],
                                        ALU.mult).then_inc(stats_step, 1)
                dve.wait_ge(stats_step, base + 3)
                nc.vector.tensor_tensor(stat[:, 1, :], stat[:, 5, :], mean_var[:, :, 1],
                                        ALU.add).then_inc(var_in, 1)

            def variance_eps(g):
                dve.wait_ge(var_out, g)
                nc.vector.tensor_scalar(stat[:, 2, :], stat_ps[:, 1, :], EPS, None,
                                        ALU.add).then_inc(var_eps, 1)

            def scales(g, keep_old):
                base = STAT_STEPS * (g - 1)
                if keep_old:
                    nc.vector.tensor_copy(norm["old"][:, :, :], norm["young"][:, :, :])
                dve.wait_ge(root_ready, g)
                nc.vector.reciprocal(stat[:, 4, :], stat[:, 3, :]).then_inc(stats_step, 1)
                dve.wait_ge(stats_step, base + 4)
                nc.vector.tensor_tensor(stat[:, 5, :], stat[:, 4, :], stat[:, 4, :],
                                        ALU.mult).then_inc(stats_step, 1)
                dve.wait_ge(stats_step, base + 5)
                nc.vector.tensor_tensor(stat[:, 3, :], stat[:, 5, :], stat[:, 2, :],
                                        ALU.mult).then_inc(stats_step, 1)
                dve.wait_ge(stats_step, base + 6)
                nc.vector.tensor_scalar(stat[:, 5, :], stat[:, 3, :], -0.5, 1.5, ALU.mult,
                                        ALU.add).then_inc(newton, 1)
                dve.wait_ge(newton, 2 * g - 1)
                nc.vector.tensor_tensor(norm["young"][:, 0, :], stat[:, 4, :], stat[:, 5, :],
                                        ALU.mult).then_inc(newton, 1)
                dve.wait_ge(newton, 2 * g)
                nc.vector.scalar_tensor_tensor(norm["young"][:, 1, :], stat_ps[:, 0, :], -1.0,
                                               norm["young"][:, 0, :], ALU.mult, ALU.mult).then_inc(scales_ready, 1)

            def finish_y(c, n):
                dve.wait_ge(shared_ready[c], n)
                dve.wait_ge(y_done[c], n)
                nc.vector.tensor_tensor(
                    y[c][:, :].rearrange("p (u two) -> p two u", two=2),
                    y_ps[c][:, 0:COLS].rearrange("p (two u) -> p two u", two=2),
                    shared[c][:, None, :].to_broadcast([C, 2, G * U]),
                    ALU.add).then_inc(y_ready[c], 1)
                dve.wait_ge(y_ready[c], n)

            def final(c, slot, r, n):
                row = x_row(c, slot, r)
                nc.vector.scalar_tensor_tensor(row, by_image(y[c]), 0.0, row, ALU.max,
                                               ALU.add).then_inc(row_final[c], 1)

            def next_input(c, carry, n, before, result=None):
                if before:
                    dve.wait_ge(d_low_ready[before[0]], before[1])
                dve.wait_ge(norm_ready[c], n)
                interior = q_row[:, :, PAD:PAD + W]
                if carry is None:
                    nc.vector.tensor_copy(interior, by_image(x_norm[c])).then_inc(q_ready[c], 1)
                else:
                    nc.vector.scalar_tensor_tensor(interior, by_image(y[carry]), 0.0, by_image(x_norm[c]),
                                                   ALU.max, ALU.add).then_inc(q_ready[c], 1)
                dve.wait_ge(q_ready[c], n)
                nc.vector.tensor_tensor(d_row[:, :, PAD - 2:PAD + W], q_row[:, :, PAD - 2:PAD + W],
                                        q_row[:, :, PAD - 1:PAD + W + 1], ALU.subtract).then_inc(d_ready[c], 1)
                if result:
                    final(c, *result)
                dve.wait_ge(q_high_ready[c], n)
                a = PAIRS // 2
                nc.vector.tensor_tensor(q_low[c][:, :, :, a:a + U], parities(q_row, PAD, W),
                                        q_high[c][:, :, :, a:a + U].bitcast(f32),
                                        ALU.subtract).then_inc(q_low_ready[c], 1)
                if result:
                    dve.wait_ge(row_final[c], result[2])
                dve.wait_ge(d_high_ready[c], n)
                nc.vector.tensor_tensor(d_low[c][:, :, :, a - 1:a + U], parities(d_row, PAD - 2, W + 2),
                                        d_high[c][:, :, :, a - 1:a + U].bitcast(f32),
                                        ALU.subtract).then_inc(d_low_ready[c], 1)

            for k in range(2):
                for n, chain in enumerate(CHAINS):
                    dve.wait_ge(first_loaded[2 * k + n], 16)
                    with dve.Fori(0, G) as b:
                        last = bn_chunk(chain, k, k, b)
                        if n == 1:
                            last.then_inc(bn_taken, 1)
            dve.wait_ge(bn_taken, 2 * G)
            channel_stats(1)
            group_variance(1)
            variance_eps(1)
            scales(1, False)
            dve.wait_ge(pads_cleared, 1)
            next_input("young", None, 1, None)

            def period(i, young, old, ahead):
                for k in range(2):
                    p = 2 * i + k
                    ny, no = HALF * i + CHUNK * k + 1, HALF * (i - 1) + CHUNK * k + 1

                    def step(r, stats):
                        if stats:
                            b = r - STATS_ROWS[0]
                            dve.wait_ge(chunk_loaded["young"], 16 * (p + 1))
                            bn_chunk("young", chunk_of("young", p + 2), k, b)
                            dve.wait_ge(chunk_loaded["old"], 16 * (p + 1))
                            bn_chunk("old", (p + 2) % OLD_SLOTS, k, b)
                        if young:
                            n = ny + r
                            finish_y("young", n)
                            next_input("young", "young", n + 1, ("old", no + r) if old else ("young", n),
                                       (chunk_of("young", p), r, n))
                        if old:
                            n = no + r
                            finish_y("old", n)
                            next_input("old", "old", n + 1, ("young", ny + r + 1) if young else ("old", n),
                                       (chunk_of("old", p), r, n))

                    if ahead:
                        with dve.Fori(0, STATS_ROWS[0]) as r:
                            step(r, False)
                        with dve.Fori(*STATS_ROWS) as r:
                            step(r, True)
                    else:
                        with dve.Fori(0, CHUNK - 1) as r:
                            step(r, False)

                    r = CHUNK - 1
                    if k == 0:
                        step(r, False)
                        continue
                    ny, no = ny + r, no + r
                    if ahead:
                        channel_stats(i + 2)
                        group_variance(i + 2)
                    before = ("old", no) if old else ("young", ny)
                    if young:
                        finish_y("young", ny)
                        final("young", chunk_of("young", p), r, ny)
                        if ahead:
                            variance_eps(i + 2)
                            scales(i + 2, True)
                            next_input("young", None, ny + 1, before)
                            before = ("young", ny + 1)
                        else:
                            nc.vector.tensor_copy(norm["old"][:, :, :],
                                                  norm["young"][:, :, :]).then_inc(scales_ready, 1)
                        dve.wait_ge(row_final["young"], ny)
                    if old:
                        finish_y("old", no)
                        final("old", chunk_of("old", p), r, no)
                    if young:
                        next_input("old", "young", no + 1, before)
                    if old:
                        dve.wait_ge(row_final["old"], no)

            period(0, True, False, True)
            with dve.Fori(1, GROUPS - 1) as i:
                period(i, True, True, True)
            period(GROUPS - 1, True, True, False)
            period(GROUPS, False, True, False)


def kernel(x, L0_conv_kernel, L0_conv_bias):
    import numpy as np
    import concourse.bacc as bacc
    from concourse import mybir
    from concourse.bass_utils import run_bass_kernel_spmd

    nc = bacc.Bacc("TRN2", target_bir_lowering=False, num_devices=1)
    arrays, args = {}, []
    for name, a in (("x", x), ("taps", L0_conv_kernel), ("bias", L0_conv_bias)):
        a = np.ascontiguousarray(a)
        arrays[f"in_{name}"] = a
        args.append(nc.dram_tensor(f"in_{name}", a.shape, mybir.dt.from_np(a.dtype), kind="ExternalInput").ap())
    out = nc.dram_tensor("out", arrays["in_x"].shape, mybir.dt.float32, kind="ExternalOutput").ap()
    conv_scan_kernel(nc, *args, out)
    r = run_bass_kernel_spmd(nc, [arrays], core_ids=[0])
    return r.results[0]["out"]
```

```python
import concourse.bass as bass
from concourse import mybir
from contextlib import ExitStack


def conv_scan_kernel(nc: bass.Bass, x: bass.AP, taps: bass.AP, bias: bass.AP, out: bass.AP):
    f32 = mybir.dt.float32
    f32r = mybir.dt.float32r
    ALU = mybir.AluOpType
    ACT = mybir.ActivationFunctionType

    IMAGES, C, H, W = x.shape
    TAPS = taps.shape[1]
    PAD = TAPS // 2
    NORM_GROUP = 4
    EPS = 1e-5

    G = 5
    GROUPS = -(-IMAGES // G)
    HALF = H // 2
    CHUNK = HALF // 2
    STATS_ROWS = (2, 2 + G)
    COLS = G * W
    U = W // 2
    PAIRS = TAPS // 2
    Q = W + 2 * PAD
    V = Q // 2
    STORED_ROWS = ((0, 6), (6, 9))
    YOUNG_SLOTS, OLD_SLOTS = 3, 5
    BN = CHUNK * W // 2
    BN_PER_IMAGE = 4 * 2
    EVEN_W, ODD_W, SUM_W, LAST_W = 0, PAIRS, 2 * PAIRS, 3 * PAIRS
    WEIGHTS = 3 * PAIRS + 1
    CHAINS = ("young", "old")

    x_view = x.rearrange("b c h w -> c b (h w)")
    out_view = out.rearrange("b c h w -> c b (h w)")

    def first_image(g):
        return 0 if isinstance(g, int) and g == 0 else g * G - (G * GROUPS - IMAGES)

    ctx = ExitStack()
    with ctx:
        def sb(name, shape, dt=f32):
            return ctx.enter_context(nc.sbuf_tensor(name, shape, dt))

        def sem(name):
            return ctx.enter_context(nc.semaphore(name))

        def pair_of(make, name):
            return {c: make(f"{name}_{c}") for c in CHAINS}

        x_young = sb("x_young", [C, YOUNG_SLOTS, G, CHUNK * W])
        x_old = sb("x_old", [C, OLD_SLOTS, G, CHUNK * W])
        x_ring = {"young": (x_young, YOUNG_SLOTS), "old": (x_old, OLD_SLOTS)}

        w_high = sb("w_high", [C, WEIGHTS, C], f32r)
        w_low = sb("w_low", [C, WEIGHTS, C], f32r)
        bias_col = sb("bias_col", [C, 1])

        y = pair_of(lambda n: sb(n, [C, COLS]), "y")
        shared = pair_of(lambda n: sb(n, [C, G * U]), "shared")
        x_norm = pair_of(lambda n: sb(n, [C, COLS]), "x_norm")
        qd_row = sb("qd_row", [C, 2, G, Q])
        q_row, d_row = qd_row[:, 0, :, :], qd_row[:, 1, :, :]
        high = pair_of(lambda n: sb(n, [C, 2, 2, G, V], f32r), "high")
        low = pair_of(lambda n: sb(n, [C, 2, 2, G, V], f32r), "low")

        group_mean = sb("group_mean", [C, C])
        bn = sb("bn", [C, G, BN_PER_IMAGE * 6])
        mean_var = sb("mean_var", [C, G, 2])
        stat = sb("stat", [C, 6, G])
        norm = pair_of(lambda n: sb(n, [C, 2, G]), "norm")
        norm_next = sb("norm_next", [C, 2, G])

        y_ps = pair_of(lambda n: ctx.enter_context(nc.psum_tensor(n, [C, 512], f32)), "y_ps")
        sum_ps = pair_of(lambda n: ctx.enter_context(nc.psum_tensor(n, [C, 512], f32)), "sum_ps")
        stat_ps = ctx.enter_context(nc.psum_tensor("stat_ps", [C, 2, G], f32))

        spare = x_young[:, YOUNG_SLOTS - 1, :, :].rearrange("p g n -> p (g n)")
        w_raw = spare[:, 0:TAPS * C].rearrange("p (k o) -> p k o", k=TAPS)
        w_sum = spare[:, TAPS * C:(TAPS + PAIRS) * C].rearrange("p (k o) -> p k o", k=PAIRS)

        weights_loaded = sem("weights_loaded")
        first_loaded = [sem(f"first_loaded{n}") for n in range(4)]
        chunk_loaded = pair_of(sem, "chunk_loaded")
        chunk_stored = pair_of(sem, "chunk_stored")
        mask_cleared = sem("mask_cleared")
        mask_ready = sem("mask_ready")
        pads_cleared = sem("pads_cleared")
        sums_made = sem("sums_made")
        high_made = sem("high_made")
        weights_ready = sem("weights_ready")
        sum_done = pair_of(sem, "sum_done")
        y_done = pair_of(sem, "y_done")
        shared_ready = pair_of(sem, "shared_ready")
        norm_ready = pair_of(sem, "norm_ready")
        y_ready = pair_of(sem, "y_ready")
        q_ready = pair_of(sem, "q_ready")
        d_ready = pair_of(sem, "d_ready")
        high_ready = pair_of(sem, "high_ready")
        low_ready = pair_of(sem, "low_ready")
        row_final = pair_of(sem, "row_final")
        bn_taken = sem("bn_taken")
        stats_step = sem("stats_step")
        scales_kept = sem("scales_kept")
        mean_in = sem("mean_in")
        mean_out = sem("mean_out")
        var_in = sem("var_in")
        var_out = sem("var_out")
        var_eps = sem("var_eps")
        root_ready = sem("root_ready")
        scales_ready = sem("scales_ready")

        block = ctx.enter_context(nc.Block())

        def chunk_of(chain, phase):
            ring, slots = x_ring[chain]
            return (phase if chain == "young" else phase - 2) % slots

        def x_row(chain, slot, r):
            ring, _ = x_ring[chain]
            return ring[:, bass.ds(slot, 1), :, bass.ds(r * W, W)].rearrange("p s g w -> p (s g) w")

        def by_image(a):
            return a[:, :].rearrange("p (g w) -> p g w", g=G)

        S0, V0, VN = PAD - 2, (PAD - 2) // 2, U + 1

        def by_parity(part):
            return qd_row[:, part, :, S0:S0 + 2 * VN].rearrange("p g (v two) -> p two g v", two=2)

        def operand(a, part):
            return a[:, :, part, :, V0:V0 + VN]

        Q_PART, D_PART = -1, 0

        STAT_STEPS = 9

        @block.sync
        def _(sp):
            sp.dma_start(w_raw, taps.rearrange("c k one o -> c k (one o)")).then_inc(weights_loaded, 16)
            sp.dma_start(bias_col[:, :], bias.rearrange("(c one) -> c one", one=1)).then_inc(weights_loaded, 16)

            def load(chain, phase, group, k, done):
                ring, slots = x_ring[chain]
                row = k * CHUNK + (HALF if chain == "old" else 0)
                sp.dma_start(
                    ring[:, bass.ds(phase % slots, 1), :, :].rearrange("p s g n -> p (s g) n"),
                    x_view[:, bass.ds(first_image(group), G), row * W:(row + CHUNK) * W],
                ).then_inc(done, 16)

            for k in range(2):
                load("young", k, 0, k, first_loaded[2 * k])
                load("old", k, 0, k, first_loaded[2 * k + 1])

            STORED = 16 * len(STORED_ROWS)

            def store(chain, phase, group, k, first, end):
                ring, slots = x_ring[chain]
                row = k * CHUNK + (HALF if chain == "old" else 0)
                sp.dma_start(
                    out_view[:, bass.ds(first_image(group), G), (row + first) * W:(row + end) * W],
                    ring[:, bass.ds(chunk_of(chain, phase), 1), :, first * W:end * W]
                    .rearrange("p s g n -> p (s g) n"),
                ).then_inc(chunk_stored[chain], 16)

            def period(i, young, old, ahead):
                for k in range(2):
                    p = 2 * i + k
                    if ahead:
                        if isinstance(i, int) and p == 0:
                            sp.wait_ge(weights_ready, 1)
                        else:
                            sp.wait_ge(chunk_stored["young"], STORED * p)
                        if not isinstance(i, int) or p > 2:
                            sp.wait_ge(chunk_stored["old"], STORED * (p - 2))
                        load("young", p + 2, i + 1, k, chunk_loaded["young"])
                        load("old", p + 2, i + 1, k, chunk_loaded["old"])
                    for first, end in STORED_ROWS:
                        if young:
                            sp.wait_ge(row_final["young"], 1 + HALF * i + CHUNK * k + end)
                            store("young", p, i, k, first, end)
                        if old:
                            sp.wait_ge(row_final["old"], 1 + HALF * (i - 1) + CHUNK * k + end)
                            store("old", p, i - 1, k, first, end)

            period(0, True, False, True)
            period(1, True, True, True)
            with sp.Fori(2, GROUPS - 1) as i:
                period(i, True, True, True)
            period(GROUPS - 1, True, True, False)
            period(GROUPS, False, True, False)
            sp.wait_ge(chunk_stored["young"], STORED * 2 * GROUPS)
            sp.wait_ge(chunk_stored["old"], STORED * 2 * GROUPS)

        @block.gpsimd
        def _(pool):
            nc.gpsimd.memset(group_mean[:, :], 1.0 / NORM_GROUP).then_inc(mask_cleared, 1)
            blocks = group_mean[:, :].rearrange("p (a b) -> p a b", b=NORM_GROUP)
            pool.wait_ge(mask_cleared, 1)
            nc.gpsimd.affine_select(out=blocks, in_=blocks, compare_op=ALU.is_ge, fill=0.0, base=0,
                                    pattern=[[-NORM_GROUP, C // NORM_GROUP], [0, NORM_GROUP]],
                                    channel_multiplier=1).then_inc(mask_cleared, 1)
            pool.wait_ge(mask_cleared, 2)
            nc.gpsimd.affine_select(out=blocks, in_=blocks, compare_op=ALU.is_ge, fill=0.0,
                                    base=NORM_GROUP - 1,
                                    pattern=[[NORM_GROUP, C // NORM_GROUP], [0, NORM_GROUP]],
                                    channel_multiplier=-1).then_inc(mask_ready, 1)

        @block.tensor
        def _(pe):
            def products(bank, weight, moving, start=False, stop=False):
                return nc.tensor.matmul(bank, weight, moving, start=start, stop=stop,
                                        skip_group_check=True)

            def row(c, n, meanwhile=None):
                even, odd = y_ps[c][:, 0:G * U], y_ps[c][:, G * U:COLS]
                both, total = y_ps[c][:, 0:COLS], sum_ps[c][:, 0:G * U]

                def shared_sum(w, moving, start=False, stop=False):
                    for j in range(PAIRS):
                        last = products(total, w[:, SUM_W + j, :], moving[:, 1, 0, :, j:j + U],
                                        start and j == 0, stop and j == PAIRS - 1)
                    return last

                def last_tap(w, moving, start=False):
                    products(both, w[:, LAST_W, :], moving[:, :, 0, :, PAIRS:PAIRS + U], start)

                def differences(w, moving, stop=False):
                    for j in range(PAIRS):
                        products(even, w[:, EVEN_W + j, :], moving[:, 0, 1, :, j:j + U])
                        last = products(odd, w[:, ODD_W + j, :], moving[:, 1, 1, :, j:j + U],
                                        stop=stop and j == PAIRS - 1)
                    return last

                pe.wait_ge(high_ready[c], 2 * n + Q_PART)
                shared_sum(w_high, high[c], start=True)
                last_tap(w_high, high[c], start=True)
                shared_sum(w_low, high[c])
                last_tap(w_low, high[c])
                pe.wait_ge(low_ready[c], 2 * n + Q_PART)
                shared_sum(w_high, low[c], stop=True).then_inc(sum_done[c], 1)
                last_tap(w_high, low[c])
                if meanwhile:
                    meanwhile()
                pe.wait_ge(high_ready[c], 2 * n + D_PART)
                differences(w_high, high[c])
                differences(w_low, high[c])
                pe.wait_ge(low_ready[c], 2 * n + D_PART)
                differences(w_high, low[c], stop=True).then_inc(y_done[c], 1)

            def average_means(g):
                pe.wait_ge(mean_in, g)
                nc.tensor.matmul(stat_ps[:, 0, :], group_mean[:, :], stat[:, 0, :],
                                 start=True, stop=True).then_inc(mean_out, 1)

            def average_variances(g):
                pe.wait_ge(var_in, g)
                nc.tensor.matmul(stat_ps[:, 1, :], group_mean[:, :], stat[:, 1, :],
                                 start=True, stop=True).then_inc(var_out, 1)

            pe.wait_ge(mask_ready, 1)
            average_means(1)
            average_variances(1)
            pe.wait_ge(weights_ready, 1)

            def period(i, young, old, ahead):
                for k in range(2):
                    with pe.Fori(0, CHUNK - 1) as r:
                        plain(i, k, r, young, old)
                    if k == 1 and ahead:
                        average_means(i + 2)
                        row("young", HALF * i + HALF, lambda: average_variances(i + 2))
                        if old:
                            row("old", HALF * (i - 1) + HALF)
                    else:
                        plain(i, k, CHUNK - 1, young, old)

            def plain(i, k, r, young, old):
                if young:
                    row("young", HALF * i + CHUNK * k + r + 1)
                if old:
                    row("old", HALF * (i - 1) + CHUNK * k + r + 1)

            period(0, True, False, True)
            with pe.Fori(1, GROUPS - 1) as i:
                period(i, True, True, True)
            period(GROUPS - 1, True, True, False)
            period(GROUPS, False, True, False)

        @block.scalar
        def _(act):
            def normalise(c, slot, r, scales):
                row = x_row(c, slot, r)
                for b in range(G):
                    last = nc.scalar.activation(by_image(x_norm[c])[:, b, :], row[:, b, :], ACT.Identity,
                                                scale=norm[scales][:, 0, b:b + 1],
                                                bias=norm[scales][:, 1, b:b + 1])
                last.then_inc(norm_ready[c], 1)

            def high_parts(c, n):
                for part, ready in enumerate((q_ready, d_ready)):
                    act.wait_ge(ready[c], n)
                    nc.scalar.activation(operand(high[c], part), by_parity(part),
                                         ACT.Copy).then_inc(high_ready[c], 1)

            def share(c, n):
                act.wait_ge(sum_done[c], n)
                nc.scalar.activation(shared[c][:, :], sum_ps[c][:, 0:G * U], ACT.Identity,
                                     bias=bias_col[:, 0:1]).then_inc(shared_ready[c], 1)

            def roots(g):
                act.wait_ge(var_eps, g)
                nc.scalar.activation(stat[:, 3, :], stat[:, 2, :], ACT.Sqrt).then_inc(root_ready, 1)

            roots(1)
            act.wait_ge(weights_loaded, 32)
            act.wait_ge(scales_ready, 1)
            act.wait_ge(pads_cleared, 1)
            normalise("young", 0, 0, "young")
            high_parts("young", 1)
            share("young", 1)
            normalise("young", 0, 1, "young")

            def period(i, young, old, ahead):
                for k in range(2):
                    p = 2 * i + k
                    ny, no = HALF * i + CHUNK * k + 1, HALF * (i - 1) + CHUNK * k + 1

                    def step(r, y_next, o_next, last_stats=False):
                        if young:
                            high_parts("young", ny + r + 1)
                            share(*(("old", no + r) if old else ("young", ny + r + 1)))
                            if y_next:
                                normalise("young", *y_next)
                        if last_stats:
                            roots(i + 2)
                        if old:
                            high_parts("old", no + r + 1)
                            share(*(("young", ny + r + 1) if young else ("old", no + r + 1)))
                        if o_next:
                            normalise("old", *o_next)

                    def rows(slot_phase, r, on, c):
                        return (chunk_of(c, slot_phase), r, c) if on else None

                    with act.Fori(0, CHUNK - 2) as r:
                        step(r, rows(p, r + 2, young, "young"), rows(p, r + 2, old, "old"))
                    if k == 0:
                        for r in (CHUNK - 2, CHUNK - 1):
                            step(r, rows(p + 1, r + 2 - CHUNK, young, "young"),
                                 rows(p + 1, r + 2 - CHUNK, old, "old"))
                        continue
                    r = CHUNK - 2
                    step(r, None, (chunk_of("old", p + 1), 0, "young") if young else None, ahead)
                    r = CHUNK - 1
                    if young and old:
                        share("old", no + r)
                    if young:
                        act.wait_ge(scales_ready, i + 2)
                        if ahead:
                            normalise("young", chunk_of("young", p + 1), 0, "young")
                            high_parts("young", ny + r + 1)
                            normalise("young", chunk_of("young", p + 1), 1, "young")
                        high_parts("old", no + r + 1)
                        share(*(("young", ny + r + 1) if ahead else ("old", no + r + 1)))
                        normalise("old", chunk_of("old", p + 1), 1, "old")

            period(0, True, False, True)
            with act.Fori(1, GROUPS - 1) as i:
                period(i, True, True, True)
            period(GROUPS - 1, True, True, False)
            period(GROUPS, False, True, False)

        @block.vector
        def _(dve):
            def clear(a):
                return nc.vector.memset(a, 0.0)

            for c in CHAINS:
                clear(y[c][:, :]).then_inc(row_final[c], 1)
                for a in (high[c], low[c]):
                    clear(a[:, :, :, :, :].bitcast(f32))
            clear(qd_row[:, :, :, :]).then_inc(pads_cleared, 1)

            dve.wait_ge(weights_loaded, 32)
            pair = w_raw[:, 0:2 * PAIRS, :].rearrange("p (j two) o -> p two j o", two=2)
            nc.vector.tensor_tensor(w_sum, pair[:, 0, :, :], pair[:, 1, :, :], ALU.add).then_inc(sums_made, 1)
            nc.vector.tensor_copy(w_high[:, EVEN_W:EVEN_W + PAIRS, :], pair[:, 0, :, :])
            nc.vector.tensor_scalar(w_high[:, ODD_W:ODD_W + PAIRS, :], pair[:, 1, :, :], -1.0, None, ALU.mult)
            dve.wait_ge(sums_made, 1)
            nc.vector.tensor_copy(w_high[:, SUM_W:SUM_W + PAIRS, :], w_sum)
            nc.vector.tensor_copy(w_high[:, LAST_W, :], w_raw[:, TAPS - 1, :]).then_inc(high_made, 1)
            dve.wait_ge(high_made, 1)

            def low_weights(at, n, full):
                return nc.vector.tensor_tensor(w_low[:, at:at + n, :], full,
                                               w_high[:, at:at + n, :].bitcast(f32), ALU.subtract)

            low_weights(EVEN_W, PAIRS, pair[:, 0, :, :])
            for j in range(PAIRS):
                nc.vector.scalar_tensor_tensor(w_low[:, ODD_W + j, :], pair[:, 1, j, :], -1.0,
                                               w_high[:, ODD_W + j, :].bitcast(f32), ALU.mult, ALU.subtract)
            low_weights(SUM_W, PAIRS, w_sum)
            low_weights(LAST_W, 1, w_raw[:, TAPS - 1:TAPS, :]).then_inc(weights_ready, 1)

            def bn_chunk(chain, slot, k, b):
                ring, _ = x_ring[chain]
                for half in range(2):
                    at = 6 * (4 * k + 2 * (chain == "old") + half)
                    last = nc.vector.bn_stats(
                        bn[:, bass.ds(b, 1), at:at + 6].rearrange("p b s -> p (b s)"),
                        ring[:, bass.ds(slot, 1), bass.ds(b, 1), half * BN:half * BN + BN]
                        .rearrange("p s b n -> p (s b n)"))
                return last

            def channel_stats(g):
                for b in range(G):
                    last = nc.vector.bn_aggr(mean_var[:, b, :], bn[:, b, :])
                base = STAT_STEPS * (g - 1)
                last.then_inc(stats_step, 1)
                dve.wait_ge(stats_step, base + 1)
                nc.vector.tensor_copy(stat[:, 0, :], mean_var[:, :, 0]).then_inc(mean_in, 1)

            def group_variance(g):
                base = STAT_STEPS * (g - 1)
                dve.wait_ge(mean_out, g)
                nc.vector.tensor_tensor(stat[:, 4, :], mean_var[:, :, 0], stat_ps[:, 0, :],
                                        ALU.subtract).then_inc(stats_step, 1)
                dve.wait_ge(stats_step, base + 2)
                nc.vector.tensor_tensor(stat[:, 5, :], stat[:, 4, :], stat[:, 4, :],
                                        ALU.mult).then_inc(stats_step, 1)
                dve.wait_ge(stats_step, base + 3)
                nc.vector.tensor_tensor(stat[:, 1, :], stat[:, 5, :], mean_var[:, :, 1],
                                        ALU.add).then_inc(var_in, 1)

            def variance_eps(g):
                dve.wait_ge(var_out, g)
                nc.vector.tensor_scalar(stat[:, 2, :], stat_ps[:, 1, :], EPS, None,
                                        ALU.add).then_inc(var_eps, 1)

            def scales(g):
                base = STAT_STEPS * (g - 1)
                dve.wait_ge(root_ready, g)
                nc.vector.reciprocal(stat[:, 4, :], stat[:, 3, :]).then_inc(stats_step, 1)
                dve.wait_ge(stats_step, base + 4)
                nc.vector.tensor_tensor(stat[:, 5, :], stat[:, 4, :], stat[:, 4, :],
                                        ALU.mult).then_inc(stats_step, 1)
                dve.wait_ge(stats_step, base + 5)
                nc.vector.tensor_tensor(stat[:, 3, :], stat[:, 5, :], stat[:, 2, :],
                                        ALU.mult).then_inc(stats_step, 1)
                dve.wait_ge(stats_step, base + 6)
                nc.vector.tensor_scalar(stat[:, 5, :], stat[:, 3, :], -0.5, 1.5, ALU.mult,
                                        ALU.add).then_inc(stats_step, 1)
                dve.wait_ge(stats_step, base + 7)
                nc.vector.tensor_tensor(norm_next[:, 0, :], stat[:, 4, :], stat[:, 5, :],
                                        ALU.mult).then_inc(stats_step, 1)
                dve.wait_ge(stats_step, base + 8)
                nc.vector.scalar_tensor_tensor(norm_next[:, 1, :], stat_ps[:, 0, :], -1.0,
                                               norm_next[:, 0, :], ALU.mult, ALU.mult).then_inc(stats_step, 1)

            def hand_scales(g, ahead):
                if g > 1:
                    dve.wait_ge(norm_ready["old"], HALF * (g - 2) + 1)
                    last = nc.vector.tensor_copy(norm["old"][:, :, :], norm["young"][:, :, :])
                    if ahead:
                        last.then_inc(scales_kept, 1)
                        dve.wait_ge(scales_kept, g - 1)
                if ahead:
                    dve.wait_ge(stats_step, STAT_STEPS * g)
                    last = nc.vector.tensor_copy(norm["young"][:, :, :], norm_next[:, :, :])
                last.then_inc(scales_ready, 1)

            def finish_y(c, n):
                dve.wait_ge(row_final[c], n)
                dve.wait_ge(shared_ready[c], n)
                dve.wait_ge(y_done[c], n)
                nc.vector.tensor_tensor(
                    y[c][:, :].rearrange("p (u two) -> p two u", two=2),
                    y_ps[c][:, 0:COLS].rearrange("p (two u) -> p two u", two=2),
                    shared[c][:, None, :].to_broadcast([C, 2, G * U]),
                    ALU.add).then_inc(y_ready[c], 1)
                dve.wait_ge(y_ready[c], n)

            def final(c, slot, r, n):
                row = x_row(c, slot, r)
                nc.vector.scalar_tensor_tensor(row, by_image(y[c]), 0.0, row, ALU.max,
                                               ALU.add).then_inc(row_final[c], 1)

            def low_part(c, n, part, count):
                dve.wait_ge(high_ready[c], 2 * n + count)
                nc.vector.tensor_tensor(operand(low[c], part), by_parity(part),
                                        operand(high[c], part).bitcast(f32),
                                        ALU.subtract).then_inc(low_ready[c], 1)

            def next_input(c, carry, n, before, alone, result=None, meanwhile=None):
                user = before or ((c, n - 1) if result else None)
                if before:
                    low_part(*before, 1, D_PART)
                if user:
                    dve.wait_ge(low_ready[user[0]], 2 * user[1] + Q_PART)
                dve.wait_ge(norm_ready[c], n)
                interior = q_row[:, :, PAD:PAD + W]
                if carry is None:
                    nc.vector.tensor_copy(interior, by_image(x_norm[c])).then_inc(q_ready[c], 1)
                else:
                    nc.vector.scalar_tensor_tensor(interior, by_image(y[carry]), 0.0, by_image(x_norm[c]),
                                                   ALU.max, ALU.add).then_inc(q_ready[c], 1)
                if meanwhile and not alone:
                    meanwhile()
                dve.wait_ge(q_ready[c], n)
                if user:
                    dve.wait_ge(low_ready[user[0]], 2 * user[1] + D_PART)
                nc.vector.tensor_tensor(d_row[:, :, S0:PAD + W], q_row[:, :, S0:PAD + W],
                                        q_row[:, :, S0 + 1:PAD + W + 1], ALU.subtract).then_inc(d_ready[c], 1)
                if result and not alone:
                    final(c, *result)
                low_part(c, n, 0, Q_PART)
                if alone:
                    low_part(c, n, 1, D_PART)
                    if result:
                        final(c, *result)
                    if meanwhile:
                        meanwhile()

            for k in range(2):
                for n, chain in enumerate(CHAINS):
                    dve.wait_ge(first_loaded[2 * k + n], 16)
                    with dve.Fori(0, G) as b:
                        last = bn_chunk(chain, k, k, b)
                        if n == 1:
                            last.then_inc(bn_taken, 1)
            dve.wait_ge(bn_taken, 2 * G)
            channel_stats(1)
            group_variance(1)
            variance_eps(1)
            scales(1)
            hand_scales(1, True)
            dve.wait_ge(pads_cleared, 1)
            next_input("young", None, 1, None, True)

            def period(i, young, old, ahead):
                for k in range(2):
                    p = 2 * i + k
                    ny, no = HALF * i + CHUNK * k + 1, HALF * (i - 1) + CHUNK * k + 1

                    def step(r, stats=False, last_stats=False):
                        b = r - STATS_ROWS[0]

                        def bn_of(chain):
                            dve.wait_ge(chunk_loaded[chain], 16 * (p + 1))
                            ring, slots = x_ring[chain]
                            bn_chunk(chain, (p + 2) % slots, k, b)

                        def bn_of_all():
                            for chain in CHAINS:
                                bn_of(chain)

                        if young:
                            n = ny + r
                            finish_y("young", n)
                            next_input("young", "young", n + 1, ("old", no + r) if old else None, not old,
                                       (chunk_of("young", p), r, n),
                                       None if not stats else (lambda: bn_of("young")) if old else bn_of_all)
                        if last_stats:
                            channel_stats(i + 2)
                            group_variance(i + 2)
                            if not old:
                                variance_eps(i + 2)
                        if old:
                            n = no + r
                            finish_y("old", n)
                            next_input("old", "old", n + 1, ("young", ny + r + 1) if young else None, not young,
                                       (chunk_of("old", p), r, n),
                                       (lambda: bn_of("old")) if stats else
                                       (lambda: variance_eps(i + 2)) if last_stats else None)
                        if last_stats:
                            scales(i + 2)

                    if ahead:
                        with dve.Fori(0, STATS_ROWS[0]) as r:
                            step(r)
                        with dve.Fori(*STATS_ROWS) as r:
                            step(r, True)
                        step(CHUNK - 2, False, k == 1)
                    else:
                        with dve.Fori(0, CHUNK - 1) as r:
                            step(r)

                    r = CHUNK - 1
                    if k == 0:
                        step(r)
                        continue
                    ny, no = ny + r, no + r
                    owed = ("old", no) if old else None
                    if young:
                        hand_scales(i + 2, ahead)
                        finish_y("young", ny)
                        final("young", chunk_of("young", p), r, ny)
                        if ahead:
                            next_input("young", None, ny + 1, owed, False)
                            owed = ("young", ny + 1)
                        else:
                            low_part(*owed, 1, D_PART)
                            owed = None
                    if old:
                        finish_y("old", no)
                        final("old", chunk_of("old", p), r, no)
                    if young:
                        next_input("old", "young", no + 1, owed, not ahead)

            period(0, True, False, True)
            with dve.Fori(1, GROUPS - 1) as i:
                period(i, True, True, True)
            period(GROUPS - 1, True, True, False)
            period(GROUPS, False, True, False)


def kernel(x, L0_conv_kernel, L0_conv_bias):
    import numpy as np
    import concourse.bacc as bacc
    from concourse import mybir
    from concourse.bass_utils import run_bass_kernel_spmd

    nc = bacc.Bacc("TRN2", target_bir_lowering=False, num_devices=1)
    arrays, args = {}, []
    for name, a in (("x", x), ("taps", L0_conv_kernel), ("bias", L0_conv_bias)):
        a = np.ascontiguousarray(a)
        arrays[f"in_{name}"] = a
        args.append(nc.dram_tensor(f"in_{name}", a.shape, mybir.dt.from_np(a.dtype), kind="ExternalInput").ap())
    out = nc.dram_tensor("out", arrays["in_x"].shape, mybir.dt.float32, kind="ExternalOutput").ap()
    conv_scan_kernel(nc, *args, out)
    r = run_bass_kernel_spmd(nc, [arrays], core_ids=[0])
    return r.results[0]["out"]
```

```python
import concourse.bass as bass
from concourse import mybir
from contextlib import ExitStack


def conv_scan_kernel(nc: bass.Bass, x: bass.AP, taps: bass.AP, bias: bass.AP, out: bass.AP):
    f32 = mybir.dt.float32
    f32r = mybir.dt.float32r
    ALU = mybir.AluOpType
    ACT = mybir.ActivationFunctionType

    IMAGES, C, H, W = x.shape
    TAPS = taps.shape[1]
    PAD = TAPS // 2
    NORM_GROUP = 4
    EPS = 1e-5

    G = 5
    GROUPS = -(-IMAGES // G)
    HALF = H // 2
    CHUNK = HALF // 2
    STATS_ROWS = (2, 2 + G)
    COLS = G * W
    U = W // 2
    PAIRS = TAPS // 2
    Q = W + 2 * PAD
    V = Q // 2
    STORED_ROWS = ((0, 6), (6, 9))
    YOUNG_SLOTS, OLD_SLOTS = 3, 5
    BN = CHUNK * W // 2
    OLD_AT = 2 * 2 * 6
    EVEN_W, ODD_W, SUM_W, LAST_W = 0, PAIRS, 2 * PAIRS, 3 * PAIRS
    WEIGHTS = 3 * PAIRS + 1
    CHAINS = ("young", "old")

    x_view = x.rearrange("b c h w -> c b (h w)")
    out_view = out.rearrange("b c h w -> c b (h w)")

    ALL = slice(0, G)
    MISSING = G * GROUPS - IMAGES
    FIRST = slice(MISSING, G)

    def first_image(g, images):
        return g * G - MISSING + images.start

    def columns(images, width):
        return slice(images.start * width, images.stop * width)

    ctx = ExitStack()
    with ctx:
        def sb(name, shape, dt=f32):
            return ctx.enter_context(nc.sbuf_tensor(name, shape, dt))

        def sem(name):
            return ctx.enter_context(nc.semaphore(name))

        def pair_of(make, name):
            return {c: make(f"{name}_{c}") for c in CHAINS}

        x_young = sb("x_young", [C, YOUNG_SLOTS, G, CHUNK * W])
        x_old = sb("x_old", [C, OLD_SLOTS, G, CHUNK * W])
        x_ring = {"young": (x_young, YOUNG_SLOTS), "old": (x_old, OLD_SLOTS)}

        w_high = sb("w_high", [C, WEIGHTS, C], f32r)
        w_low = sb("w_low", [C, WEIGHTS, C], f32r)
        bias_col = sb("bias_col", [C, 1])

        y = pair_of(lambda n: sb(n, [C, COLS]), "y")
        shared = pair_of(lambda n: sb(n, [C, G * U]), "shared")
        x_norm = pair_of(lambda n: sb(n, [C, COLS]), "x_norm")
        qd_row = sb("qd_row", [C, 2, G, Q])
        q_row, d_row = qd_row[:, 0, :, :], qd_row[:, 1, :, :]
        high = pair_of(lambda n: sb(n, [C, 2, 2, G, V], f32r), "high")
        low = pair_of(lambda n: sb(n, [C, 2, 2, G, V], f32r), "low")

        group_mean = sb("group_mean", [C, C])
        bn = sb("bn", [C, G, OLD_AT + 2 * 3])
        minus_base = sb("minus_base", [C, 2, G])
        sums = sb("sums", [C, 2, 2, G])
        sums_work = sb("sums_work", [C, 2, 2, G])
        unused = sb("unused", [C, CHUNK * W], mybir.dt.bfloat16)
        mean_var = sb("mean_var", [C, G, 2])
        stat = sb("stat", [C, 6, G])
        norm = pair_of(lambda n: sb(n, [C, 2, G]), "norm")
        norm_next = sb("norm_next", [C, 2, G])

        y_ps = pair_of(lambda n: ctx.enter_context(nc.psum_tensor(n, [C, 2, 512], f32)), "y_ps")
        sum_ps = pair_of(lambda n: ctx.enter_context(nc.psum_tensor(n, [C, 512], f32)), "sum_ps")
        stat_ps = ctx.enter_context(nc.psum_tensor("stat_ps", [C, 512], f32))
        mean_ps, variance_ps = stat_ps[:, 0:G], stat_ps[:, G:2 * G]
        unread_ps = ctx.enter_context(nc.psum_tensor("unread_ps", [C, 512], f32))

        spare = x_young[:, YOUNG_SLOTS - 1, :, :].rearrange("p g n -> p (g n)")
        w_raw = spare[:, 0:TAPS * C].rearrange("p (k o) -> p k o", k=TAPS)
        w_sum = spare[:, TAPS * C:(TAPS + PAIRS) * C].rearrange("p (k o) -> p k o", k=PAIRS)

        weights_loaded = sem("weights_loaded")
        first_loaded = pair_of(lambda n: [[sem(f"{n}{k}_{b}") for b in range(G)] for k in range(2)],
                               "first_loaded")
        chunk_loaded = pair_of(lambda n: [sem(f"{n}{k}") for k in range(2)], "chunk_loaded")
        chunk_stored = pair_of(sem, "chunk_stored")
        mask_cleared = sem("mask_cleared")
        mask_ready = sem("mask_ready")
        pads_cleared = sem("pads_cleared")
        sums_made = sem("sums_made")
        high_made = sem("high_made")
        weights_ready = sem("weights_ready")
        sum_done = pair_of(sem, "sum_done")
        y_done = pair_of(sem, "y_done")
        shared_ready = pair_of(sem, "shared_ready")
        norm_ready = pair_of(sem, "norm_ready")
        y_ready = pair_of(sem, "y_ready")
        q_ready = pair_of(sem, "q_ready")
        d_ready = pair_of(sem, "d_ready")
        input_step = pair_of(sem, "input_step")
        even_high_ready = pair_of(sem, "even_high_ready")
        high_ready = pair_of(sem, "high_ready")
        low_ready = pair_of(sem, "low_ready")
        row_final = pair_of(sem, "row_final")
        bn_taken = sem("bn_taken")
        base_taken = sem("base_taken")
        sum_taken = sem("sum_taken")
        stats_step = sem("stats_step")
        scales_handed = sem("scales_handed")
        mean_in = sem("mean_in")
        mean_out = sem("mean_out")
        var_in = sem("var_in")
        var_out = sem("var_out")
        var_eps = sem("var_eps")
        root_ready = sem("root_ready")

        block = ctx.enter_context(nc.Block())

        def chunk_of(chain, phase):
            _, slots = x_ring[chain]
            return (phase if chain == "young" else phase - 2) % slots

        def x_row(chain, slot, r, images=ALL):
            ring, _ = x_ring[chain]
            return ring[:, bass.ds(slot, 1), images, bass.ds(r * W, W)].rearrange("p s g w -> p (s g) w")

        def by_image(a, images=ALL):
            return a[:, columns(images, W)].rearrange("p (g w) -> p g w", w=W)

        S0, V0, VN = PAD - 2, (PAD - 2) // 2, U + 1

        def by_parity(part, images):
            return qd_row[:, part, images, S0:S0 + 2 * VN].rearrange("p g (v two) -> p two g v", two=2)

        def operand(a, part, images):
            return a[:, :, part, images, V0:V0 + VN]

        Q_PART, D_PART = -1, 0
        ODD, EVEN = -1, 0

        STEPS = ("odd_high", "odd", "odd_low", "even", "d_odd_high", "d_odd", "d_even", "d_odd_low",
                 "even_low", "d_even_low")
        BEFORE_ALONE = {"young": 0, "old": HALF * (GROUPS - 1)}
        BEFORE_PAIRED = {"young": HALF, "old": 0}

        def at_step(c, n, step):
            return len(STEPS) * (lone(c, n) - 1) + STEPS.index(step) + 1

        def lone(c, n):
            return n - BEFORE_ALONE[c]

        def paired(c, n):
            return n - BEFORE_PAIRED[c]

        STAT_STEPS = 11

        @block.sync
        def _(sp):
            def load(chain, images, phase, group, k, done):
                ring, slots = x_ring[chain]
                row = k * CHUNK + (HALF if chain == "old" else 0)
                sp.dma_start(
                    ring[:, bass.ds(phase % slots, 1), images, :].rearrange("p s g n -> p (s g) n"),
                    x_view[:, bass.ds(first_image(group, images), images.stop - images.start),
                           row * W:(row + CHUNK) * W],
                ).then_inc(done, 16)

            def load_first(chain, k):
                for b in range(FIRST.start, FIRST.stop):
                    load(chain, slice(b, b + 1), k, 0, k, first_loaded[chain][k][b])

            load_first("old", 0)
            sp.dma_start(w_raw, taps.rearrange("c k one o -> c k (one o)")).then_inc(weights_loaded, 16)
            sp.dma_start(bias_col[:, :], bias.rearrange("(c one) -> c one", one=1)).then_inc(weights_loaded, 16)
            load_first("old", 1)
            load_first("young", 0)
            load_first("young", 1)

            STORED = 16 * len(STORED_ROWS)

            def store(chain, images, phase, group, k, first, end):
                ring, _ = x_ring[chain]
                row = k * CHUNK + (HALF if chain == "old" else 0)
                sp.dma_start(
                    out_view[:, bass.ds(first_image(group, images), images.stop - images.start),
                             (row + first) * W:(row + end) * W],
                    ring[:, bass.ds(chunk_of(chain, phase), 1), images, first * W:end * W]
                    .rearrange("p s g n -> p (s g) n"),
                ).then_inc(chunk_stored[chain], 16)

            def period(i, young, old, ahead):
                for k in range(2):
                    p = 2 * i + k
                    if ahead:
                        if isinstance(i, int) and p == 0:
                            sp.wait_ge(weights_ready, 1)
                        else:
                            sp.wait_ge(chunk_stored["young"], STORED * p)
                        load("young", ALL, p + 2, i + 1, k, chunk_loaded["young"][k])
                        if isinstance(i, int) and i == 0:
                            if k == 0:
                                for half in range(2):
                                    load("old", ALL, 2 + half, 1, half, chunk_loaded["old"][half])
                        else:
                            if not isinstance(i, int) or p > 2:
                                sp.wait_ge(chunk_stored["old"], STORED * (p - 2))
                            load("old", ALL, p + 2, i + 1, k, chunk_loaded["old"][k])
                    for first, end in STORED_ROWS:
                        if young:
                            sp.wait_ge(row_final["young"], 1 + HALF * i + CHUNK * k + end)
                            store("young", young, p, i, k, first, end)
                        if old:
                            sp.wait_ge(row_final["old"], 1 + HALF * (i - 1) + CHUNK * k + end)
                            store("old", old, p, i - 1, k, first, end)

            period(0, FIRST, None, True)
            period(1, ALL, FIRST, True)
            with sp.Fori(2, GROUPS - 1) as i:
                period(i, ALL, ALL, True)
            period(GROUPS - 1, ALL, ALL, False)
            period(GROUPS, None, ALL, False)
            sp.wait_ge(chunk_stored["young"], STORED * 2 * GROUPS)
            sp.wait_ge(chunk_stored["old"], STORED * 2 * GROUPS)

        @block.gpsimd
        def _(pool):
            nc.gpsimd.memset(group_mean[:, :], 1.0 / NORM_GROUP).then_inc(mask_cleared, 1)
            blocks = group_mean[:, :].rearrange("p (a b) -> p a b", b=NORM_GROUP)
            pool.wait_ge(mask_cleared, 1)
            nc.gpsimd.affine_select(out=blocks, in_=blocks, compare_op=ALU.is_ge, fill=0.0, base=0,
                                    pattern=[[-NORM_GROUP, C // NORM_GROUP], [0, NORM_GROUP]],
                                    channel_multiplier=1).then_inc(mask_cleared, 1)
            pool.wait_ge(mask_cleared, 2)
            nc.gpsimd.affine_select(out=blocks, in_=blocks, compare_op=ALU.is_ge, fill=0.0,
                                    base=NORM_GROUP - 1,
                                    pattern=[[NORM_GROUP, C // NORM_GROUP], [0, NORM_GROUP]],
                                    channel_multiplier=-1).then_inc(mask_ready, 1)

        UNTIL_STATISTICS = 96
        UNTIL_NORMALISED = 30

        @block.tensor
        def _(pe):
            def products(bank, weight, moving, start=False, stop=False):
                return nc.tensor.matmul(bank, weight, moving, start=start, stop=stop,
                                        skip_group_check=True)

            def row(c, images, n, alone, stats_of=None):
                out = columns(images, U)
                y_of = [y_ps[c][:, parity, out] for parity in range(2)]
                total = sum_ps[c][:, out]

                def shared_sum(w, moving, start=False, stop=False):
                    for j in range(PAIRS):
                        last = products(total, w[:, SUM_W + j, :], moving[:, 1, 0, images, j:j + U],
                                        start and j == 0, stop and j == PAIRS - 1)
                    return last

                def last_tap(parity, w, moving, start=False):
                    products(y_of[parity], w[:, LAST_W, :], moving[:, parity, 0, images, PAIRS:PAIRS + U],
                             start)

                def differences(parity, w, moving, stop=False):
                    at = ODD_W if parity else EVEN_W
                    for j in range(PAIRS):
                        last = products(y_of[parity], w[:, at + j, :], moving[:, parity, 1, images, j:j + U],
                                        stop=stop and j == PAIRS - 1)
                    return last

                if alone:
                    def wait_for(step):
                        pe.wait_ge(input_step[c], at_step(c, n, step))

                    wait_for("odd_high")
                    shared_sum(w_high, high[c], start=True)
                    shared_sum(w_low, high[c])
                    last_tap(1, w_high, high[c], start=True)
                    last_tap(1, w_low, high[c])
                    wait_for("odd_low")
                    shared_sum(w_high, low[c], stop=True).then_inc(sum_done[c], 1)
                    last_tap(1, w_high, low[c])
                    pe.wait_ge(even_high_ready[c], 2 * lone(c, n) + Q_PART)
                    last_tap(0, w_high, high[c], start=True)
                    last_tap(0, w_low, high[c])
                    wait_for("d_odd_high")
                    differences(1, w_high, high[c])
                    differences(1, w_low, high[c])
                    wait_for("d_odd_low")
                    differences(1, w_high, low[c], stop=True).then_inc(y_done[c], 1)
                    pe.wait_ge(even_high_ready[c], 2 * lone(c, n) + D_PART)
                    differences(0, w_high, high[c])
                    differences(0, w_low, high[c])
                    if stats_of is not None:
                        average_means(stats_of)
                    wait_for("even_low")
                    last_tap(0, w_high, low[c])
                    wait_for("d_even_low")
                    differences(0, w_high, low[c], stop=True).then_inc(y_done[c], 1)
                    if stats_of is not None:
                        average_variances(stats_of)
                    return

                pe.wait_ge(high_ready[c], 2 * paired(c, n) + Q_PART)
                shared_sum(w_high, high[c], start=True)
                for parity in (1, 0):
                    last_tap(parity, w_high, high[c], start=True)
                if stats_of is not None:
                    average_means(stats_of)
                shared_sum(w_low, high[c])
                for parity in (1, 0):
                    last_tap(parity, w_low, high[c])
                pe.wait_ge(low_ready[c], 2 * paired(c, n) + Q_PART)
                shared_sum(w_high, low[c], stop=True).then_inc(sum_done[c], 1)
                if stats_of is not None:
                    average_variances(stats_of)
                for parity in (1, 0):
                    last_tap(parity, w_high, low[c])
                pe.wait_ge(high_ready[c], 2 * paired(c, n) + D_PART)
                for parity in (1, 0):
                    differences(parity, w_high, high[c])
                for parity in (1, 0):
                    differences(parity, w_low, high[c])
                pe.wait_ge(low_ready[c], 2 * paired(c, n) + D_PART)
                for parity in (1, 0):
                    differences(parity, w_high, low[c], stop=True).then_inc(y_done[c], 1)

            def average_means(g):
                pe.wait_ge(mean_in, g)
                nc.tensor.matmul(mean_ps, group_mean[:, :], mean_var[:, :, 0],
                                 start=True, stop=True).then_inc(mean_out, 1)

            def average_variances(g):
                pe.wait_ge(var_in, g)
                nc.tensor.matmul(variance_ps, group_mean[:, :], stat[:, 1, :],
                                 start=True, stop=True).then_inc(var_out, 1)

            def stay_warm(count):
                for _ in range(count):
                    products(unread_ps[:, 0:2 * C], w_high[:, 0, :], w_high[:, 0:2, :], start=True, stop=True)

            pe.wait_ge(mask_ready, 1)
            pe.wait_ge(weights_ready, 1)
            with pe.Fori(0, 8):
                stay_warm(UNTIL_STATISTICS // 8)
            average_means(1)
            stay_warm(6)
            average_variances(1)
            stay_warm(UNTIL_NORMALISED)

            def period(i, young, old, ahead):
                for k in range(2):
                    with pe.Fori(0, CHUNK - 1) as r:
                        rows(i, k, r, young, old)
                    if k == 1 and ahead:
                        row("young", young, HALF * i + HALF, not old, i + 2)
                        if old:
                            row("old", old, HALF * (i - 1) + HALF, False)
                        else:
                            stay_warm(UNTIL_NORMALISED)
                    else:
                        rows(i, k, CHUNK - 1, young, old)

            def rows(i, k, r, young, old):
                if young:
                    row("young", young, HALF * i + CHUNK * k + r + 1, not old)
                if old:
                    row("old", old, HALF * (i - 1) + CHUNK * k + r + 1, not young)

            period(0, FIRST, None, True)
            period(1, ALL, FIRST, True)
            with pe.Fori(2, GROUPS - 1) as i:
                period(i, ALL, ALL, True)
            period(GROUPS - 1, ALL, ALL, False)
            period(GROUPS, None, ALL, False)

        @block.scalar
        def _(act):
            def normalise(c, images, slot, r, scales, whole=True):
                row = x_row(c, slot, r)
                scales = norm_next if scales == "next" else norm[scales]
                for b in range(images.start, images.stop):
                    last = nc.scalar.activation(by_image(x_norm[c])[:, b, :], row[:, b, :], ACT.Identity,
                                                scale=scales[:, 0, b:b + 1],
                                                bias=scales[:, 1, b:b + 1])
                if whole:
                    last.then_inc(norm_ready[c], 1)

            def even_high_parts(c, images, n, following=None):
                for part, step in ((0, "even"), (1, "d_even")):
                    act.wait_ge(input_step[c], at_step(c, n, step))
                    nc.scalar.activation(operand(high[c], part, images)[:, 0, :, :],
                                         by_parity(part, images)[:, 0, :, :],
                                         ACT.Copy).then_inc(even_high_ready[c], 1)
                    if part == 0 and following:
                        normalise(c, slice(images.start, images.start + 2), *following, False)

            def high_parts(c, images, n):
                for part, ready in ((0, q_ready), (1, d_ready)):
                    act.wait_ge(ready[c], paired(c, n))
                    nc.scalar.activation(operand(high[c], part, images), by_parity(part, images),
                                         ACT.Copy).then_inc(high_ready[c], 1)

            def hand_scales(g):
                if not isinstance(g, int) or g > 1:
                    nc.scalar.activation(norm["old"][:, :, :], norm["young"][:, :, :],
                                         ACT.Copy).then_inc(scales_handed, 1)
                    act.wait_ge(scales_handed, 2 * g - 2)
                if isinstance(g, int) and g > GROUPS:
                    return
                nc.scalar.activation(norm["young"][:, :, :], norm_next[:, :, :],
                                     ACT.Copy).then_inc(scales_handed, 1)
                act.wait_ge(scales_handed, 2 * g - 1)

            def share(c, images, n):
                act.wait_ge(sum_done[c], n)
                out = columns(images, U)
                nc.scalar.activation(shared[c][:, out], sum_ps[c][:, out], ACT.Identity,
                                     bias=bias_col[:, 0:1]).then_inc(shared_ready[c], 1)

            def roots(g):
                act.wait_ge(var_eps, g)
                nc.scalar.activation(stat[:, 3, :], stat[:, 2, :], ACT.Sqrt).then_inc(root_ready, 1)

            def sum_of(chunk, k, b, square, n):
                act.wait_ge(sum_taken, n)
                nc.scalar.activation(unused[:, :], chunk, ACT.Square if square else ACT.Identity,
                                     bias=minus_base[:, k, bass.ds(b, 1)],
                                     accum_out=sums[:, int(square), k, bass.ds(b, 1)]).then_inc(sum_taken, 1)

            def base_of(chunk, k, b):
                nc.scalar.activation(minus_base[:, k, bass.ds(b, 1)], chunk[:, 0:1], ACT.Copy,
                                     scale=-1.0).then_inc(base_taken, 1)

            def image_chunk(slot, b):
                return x_old[:, bass.ds(slot, 1), bass.ds(b, 1), :].rearrange("p s b n -> p (s b n)")

            act.wait_ge(sum_taken, 1)
            nc.scalar.activation(unused[:, 0:1], unused[:, 0:1], ACT.Sqrt)
            for k in range(2):
                for b in range(FIRST.start, FIRST.stop):
                    n = k * (G - MISSING) + b - MISSING
                    act.wait_ge(first_loaded["old"][k][b], 16)
                    base_of(image_chunk(k, b), k, b)
                    act.wait_ge(base_taken, n + 1)
                    sum_of(image_chunk(k, b), k, b, False, 2 * n + 1)
                    sum_of(image_chunk(k, b), k, b, True, 2 * n + 2)
            roots(1)
            act.wait_ge(weights_loaded, 32)
            act.wait_ge(pads_cleared, 1)
            act.wait_ge(stats_step, STAT_STEPS)
            normalise("young", FIRST, 0, 0, "next")
            even_high_parts("young", FIRST, 1)
            normalise("young", FIRST, 0, 1, "next")
            hand_scales(1)
            share("young", FIRST, 1)

            def period(i, young, old, ahead):
                for k in range(2):
                    p = 2 * i + k
                    ny, no = HALF * i + CHUNK * k + 1, HALF * (i - 1) + CHUNK * k + 1

                    def step(r, y_next, o_next, stats=False, last_stats=False):
                        b = r - STATS_ROWS[0]
                        n = (p + 2) * G + b - 2 * MISSING
                        chunk = image_chunk((p + 2) % OLD_SLOTS, b) if stats else None
                        alone = not (young and old)
                        if alone:
                            c, images, row = ("young", young, ny + r + 1) if young else ("old", old, no + r + 1)
                            following = y_next or o_next
                            even_high_parts(c, images, row, following)
                            share(c, images, row)
                            if following:
                                normalise(c, slice(images.start + 2, images.stop), *following)
                        else:
                            high_parts("young", young, ny + r + 1)
                            share("old", old, no + r)
                            if y_next:
                                normalise("young", young, *y_next)
                        if stats:
                            act.wait_ge(chunk_loaded["old"][k], 16 * (i + 1))
                            base_of(chunk, k, b)
                            act.wait_ge(base_taken, n + 1)
                            sum_of(chunk, k, b, False, 2 * n + 1)
                        if last_stats:
                            roots(i + 2)
                        if not alone:
                            high_parts("old", old, no + r + 1)
                            share("young", young, ny + r + 1)
                            if o_next:
                                normalise("old", old, *o_next)
                        if stats:
                            sum_of(chunk, k, b, True, 2 * n + 2)

                    def rows(slot_phase, r, on, c):
                        return (chunk_of(c, slot_phase), r, c) if on else None

                    for first, end in ((0, STATS_ROWS[0]), STATS_ROWS):
                        with act.Fori(first, end) as r:
                            step(r, rows(p, r + 2, young, "young"), rows(p, r + 2, old, "old"),
                                 ahead and first > 0)
                    if k == 0:
                        for r in (CHUNK - 2, CHUNK - 1):
                            step(r, rows(p + 1, r + 2 - CHUNK, young, "young"),
                                 rows(p + 1, r + 2 - CHUNK, old, "old"))
                        continue
                    r = CHUNK - 2
                    step(r, None, None, False, ahead)
                    r = CHUNK - 1
                    if young and ahead:
                        act.wait_ge(stats_step, STAT_STEPS * (i + 2))
                        normalise("young", ALL, chunk_of("young", p + 1), 0, "next")
                    if young and not ahead:
                        normalise("old", young, chunk_of("old", p + 1), 0, "young")
                    if young and old:
                        share("old", old, no + r)
                    if young:
                        if ahead:
                            high_parts("young", ALL, ny + r + 1)
                            normalise("old", young, chunk_of("old", p + 1), 0, "young")
                            share("young", ALL, ny + r + 1)
                        (high_parts if ahead else even_high_parts)("old", young, no + r + 1)
                        hand_scales(i + 2)
                        if ahead:
                            normalise("young", ALL, chunk_of("young", p + 1), 1, "young")
                        normalise("old", young, chunk_of("old", p + 1), 1, "old")
                        if not ahead:
                            share("old", young, no + r + 1)

            period(0, FIRST, None, True)
            period(1, ALL, FIRST, True)
            with act.Fori(2, GROUPS - 1) as i:
                period(i, ALL, ALL, True)
            period(GROUPS - 1, ALL, ALL, False)
            period(GROUPS, None, ALL, False)

        @block.vector
        def _(dve):
            def clear(a):
                return nc.vector.memset(a, 0.0)

            clear(unused[:, :]).then_inc(sum_taken, 1)
            for c in CHAINS:
                clear(y[c][:, :]).then_inc(row_final[c], 1)
                for a in (high[c], low[c]):
                    clear(a[:, :, :, :, :].bitcast(f32))
            nc.vector.memset(bn[:, 0:MISSING, 0:OLD_AT], 1.0)
            clear(sums[:, :, :, 0:MISSING])
            clear(minus_base[:, :, 0:MISSING])
            clear(qd_row[:, :, :, :]).then_inc(pads_cleared, 1)

            dve.wait_ge(weights_loaded, 32)
            pair = w_raw[:, 0:2 * PAIRS, :].rearrange("p (j two) o -> p two j o", two=2)
            nc.vector.tensor_tensor(w_sum, pair[:, 0, :, :], pair[:, 1, :, :], ALU.add).then_inc(sums_made, 1)
            nc.vector.tensor_copy(w_high[:, EVEN_W:EVEN_W + PAIRS, :], pair[:, 0, :, :])
            nc.vector.tensor_scalar(w_high[:, ODD_W:ODD_W + PAIRS, :], pair[:, 1, :, :], -1.0, None, ALU.mult)
            dve.wait_ge(sums_made, 1)
            nc.vector.tensor_copy(w_high[:, SUM_W:SUM_W + PAIRS, :], w_sum)
            nc.vector.tensor_copy(w_high[:, LAST_W, :], w_raw[:, TAPS - 1, :]).then_inc(high_made, 1)
            dve.wait_ge(high_made, 1)

            def low_weights(at, n, full):
                return nc.vector.tensor_tensor(w_low[:, at:at + n, :], full,
                                               w_high[:, at:at + n, :].bitcast(f32), ALU.subtract)

            low_weights(EVEN_W, PAIRS, pair[:, 0, :, :])
            for j in range(PAIRS):
                nc.vector.scalar_tensor_tensor(w_low[:, ODD_W + j, :], pair[:, 1, j, :], -1.0,
                                               w_high[:, ODD_W + j, :].bitcast(f32), ALU.mult, ALU.subtract)
            low_weights(SUM_W, PAIRS, w_sum)
            low_weights(LAST_W, 1, w_raw[:, TAPS - 1:TAPS, :]).then_inc(weights_ready, 1)

            def bn_half(slot, k, b, half):
                at = 6 * (2 * k + half)
                return nc.vector.bn_stats(
                    bn[:, bass.ds(b, 1), at:at + 6].rearrange("p b s -> p (b s)"),
                    x_young[:, bass.ds(slot, 1), bass.ds(b, 1), half * BN:half * BN + BN]
                    .rearrange("p s b n -> p (s b n)"))

            def mean_of_sums(g):
                dve.wait_ge(sum_taken, 1 + 2 * 2 * (G * g - MISSING))
                nc.vector.tensor_scalar(sums_work[:, 0, :, :], sums[:, 0, :, :], 1.0 / (CHUNK * W), None,
                                        ALU.mult).then_inc(stats_step, 1)

            def square_of_sums(g):
                by_chunk = bn[:, :, OLD_AT:OLD_AT + 6].rearrange("p g (k s) -> p s k g", k=2)
                dve.wait_ge(stats_step, STAT_STEPS * (g - 1) + 1)
                nc.vector.tensor_tensor(sums_work[:, 1, :, :], sums[:, 0, :, :], sums_work[:, 0, :, :],
                                        ALU.mult).then_inc(stats_step, 1)
                nc.vector.tensor_tensor(by_chunk[:, 1, :, :], sums_work[:, 0, :, :], minus_base[:, :, :],
                                        ALU.subtract)

            def variance_of_sums(g):
                by_chunk = bn[:, :, OLD_AT:OLD_AT + 6].rearrange("p g (k s) -> p s k g", k=2)
                dve.wait_ge(stats_step, STAT_STEPS * (g - 1) + 2)
                nc.vector.tensor_tensor(by_chunk[:, 2, :, :], sums[:, 1, :, :], sums_work[:, 1, :, :],
                                        ALU.subtract).then_inc(stats_step, 1)

            def channel_stats(g):
                dve.drain()
                for b in range(G):
                    last = nc.vector.bn_aggr(mean_var[:, b, :], bn[:, b, :])
                last.then_inc(mean_in, 1)

            def group_variance(g):
                base = STAT_STEPS * (g - 1)
                dve.wait_ge(mean_out, g)
                nc.vector.tensor_tensor(stat[:, 4, :], mean_var[:, :, 0], mean_ps,
                                        ALU.subtract).then_inc(stats_step, 1)
                dve.wait_ge(stats_step, base + 4)
                nc.vector.tensor_tensor(stat[:, 5, :], stat[:, 4, :], stat[:, 4, :],
                                        ALU.mult).then_inc(stats_step, 1)
                dve.wait_ge(stats_step, base + 5)
                nc.vector.tensor_tensor(stat[:, 1, :], stat[:, 5, :], mean_var[:, :, 1],
                                        ALU.add).then_inc(var_in, 1)

            def variance_eps(g):
                dve.wait_ge(var_out, g)
                nc.vector.tensor_scalar(stat[:, 2, :], variance_ps, EPS, None,
                                        ALU.add).then_inc(var_eps, 1)

            def inverse_root(g):
                dve.wait_ge(root_ready, g)
                nc.vector.reciprocal(stat[:, 4, :], stat[:, 3, :]).then_inc(stats_step, 1)

            def its_square(g):
                dve.wait_ge(stats_step, STAT_STEPS * (g - 1) + 6)
                nc.vector.tensor_tensor(stat[:, 5, :], stat[:, 4, :], stat[:, 4, :],
                                        ALU.mult).then_inc(stats_step, 1)

            def times_variance(g):
                dve.wait_ge(stats_step, STAT_STEPS * (g - 1) + 7)
                nc.vector.tensor_tensor(stat[:, 3, :], stat[:, 5, :], stat[:, 2, :],
                                        ALU.mult).then_inc(stats_step, 1)

            def scale_and_shift(g):
                base = STAT_STEPS * (g - 1)
                dve.wait_ge(stats_step, base + 8)
                nc.vector.tensor_scalar(stat[:, 5, :], stat[:, 3, :], -0.5, 1.5, ALU.mult,
                                        ALU.add).then_inc(stats_step, 1)
                dve.wait_ge(stats_step, base + 9)
                nc.vector.tensor_tensor(norm_next[:, 0, :], stat[:, 4, :], stat[:, 5, :],
                                        ALU.mult).then_inc(stats_step, 1)
                dve.wait_ge(stats_step, base + 10)
                nc.vector.scalar_tensor_tensor(norm_next[:, 1, :], mean_ps, -1.0,
                                               norm_next[:, 0, :], ALU.mult, ALU.mult).then_inc(stats_step, 1)

            def finish_y(c, images, n):
                out = columns(images, U)
                y_at = y[c][:, columns(images, W)].rearrange("p (u two) -> p two u", two=2)
                dve.wait_ge(row_final[c], n)
                dve.wait_ge(shared_ready[c], n)
                dve.wait_ge(y_done[c], 2 * n + EVEN)
                nc.vector.tensor_tensor(y_at, y_ps[c][:, :, out],
                                        shared[c][:, None, out].to_broadcast([C, 2, out.stop - out.start]),
                                        ALU.add).then_inc(y_ready[c], 2)

            def final(c, images, slot, r, n):
                row = x_row(c, slot, r, images)
                nc.vector.scalar_tensor_tensor(row, by_image(y[c], images), 0.0, row, ALU.max,
                                               ALU.add).then_inc(row_final[c], 1)

            def low_part(c, images, n, part, count):
                dve.wait_ge(high_ready[c], 2 * paired(c, n) + count)
                nc.vector.tensor_tensor(operand(low[c], part, images), by_parity(part, images),
                                        operand(high[c], part, images).bitcast(f32),
                                        ALU.subtract).then_inc(low_ready[c], 1)

            def low_of_earlier(before):
                if before:
                    low_part(*before, 1, D_PART)

            def input_row(c, images, carry, n, before):
                if before:
                    dve.wait_ge(low_ready[before[0]], 2 * paired(before[0], before[2]) + Q_PART)
                dve.wait_ge(norm_ready[c], n)
                interior = q_row[:, images, PAD:PAD + W]
                if carry is None:
                    nc.vector.tensor_copy(interior, by_image(x_norm[c], images)).then_inc(q_ready[c], 1)
                else:
                    carry, count = carry
                    dve.wait_ge(y_ready[carry], 2 * count)
                    nc.vector.scalar_tensor_tensor(interior, by_image(y[carry], images), 0.0,
                                                   by_image(x_norm[c], images),
                                                   ALU.max, ALU.add).then_inc(q_ready[c], 1)

            def input_differences(c, images, n, before):
                dve.wait_ge(q_ready[c], paired(c, n))
                if before:
                    dve.wait_ge(low_ready[before[0]], 2 * paired(before[0], before[2]) + D_PART)
                nc.vector.tensor_tensor(d_row[:, images, S0:PAD + W], q_row[:, images, S0:PAD + W],
                                        q_row[:, images, S0 + 1:PAD + W + 1], ALU.subtract).then_inc(d_ready[c], 1)

            def finish_parity(c, images, n, parity):
                out = columns(images, U)
                y_at = y[c][:, columns(images, W)].rearrange("p (u two) -> p two u", two=2)
                dve.wait_ge(y_done[c], 2 * n + (ODD if parity else EVEN))
                if parity:
                    dve.wait_ge(row_final[c], n)
                nc.vector.tensor_tensor(y_at[:, parity, :], y_ps[c][:, parity, out],
                                        shared[c][:, out], ALU.add).then_inc(y_ready[c], 1)

            def input_alone(c, images, carry, n, carry_is_odd=False):
                def wait_for(step):
                    dve.wait_ge(input_step[c], at_step(c, n, step))

                def sample(parity, place):
                    def of_parity(a):
                        return by_image(a, images).rearrange("p g (u two) -> p two g u", two=2)[:, parity, :, :]

                    if carry is None:
                        return nc.vector.tensor_copy(place, of_parity(x_norm[c]))
                    dve.wait_ge(y_ready[carry[0]], 2 * carry[1] + (ODD if parity else EVEN))
                    return nc.vector.scalar_tensor_tensor(place, of_parity(y[carry[0]]), 0.0,
                                                          of_parity(x_norm[c]), ALU.max, ALU.add)

                def full_place(parity):
                    return q_row[:, images, PAD:PAD + W].rearrange("p g (u two) -> p two g u", two=2)[:, parity, :, :]

                def difference(parity, place):
                    right = (qd_row[:, 0, images, S0 + 1:S0 + 1 + 2 * VN]
                             .rearrange("p g (v two) -> p two g v", two=2))
                    return nc.vector.tensor_tensor(place[:, parity, :, :], by_parity(0, images)[:, parity, :, :],
                                                   right[:, parity, :, :], ALU.subtract)

                def low_of(part, parity):
                    return nc.vector.tensor_tensor(operand(low[c], part, images)[:, parity, :, :],
                                                   by_parity(part, images)[:, parity, :, :],
                                                   operand(high[c], part, images).bitcast(f32)[:, parity, :, :],
                                                   ALU.subtract)

                sample(1, high[c][:, 1, 0, images, PAD // 2:PAD // 2 + U]).then_inc(input_step[c], 1)
                sample(1, full_place(1)).then_inc(input_step[c], 1)
                if carry_is_odd:
                    finish_parity(c, images, n - 1, 0)
                wait_for("odd")
                low_of(0, 1).then_inc(input_step[c], 1)
                sample(0, full_place(0)).then_inc(input_step[c], 1)
                wait_for("even")
                difference(1, operand(high[c], 1, images)).then_inc(input_step[c], 1)
                difference(1, by_parity(1, images)).then_inc(input_step[c], 1)
                difference(0, by_parity(1, images)).then_inc(input_step[c], 1)
                wait_for("d_odd")
                low_of(1, 1).then_inc(input_step[c], 1)
                dve.wait_ge(even_high_ready[c], 2 * lone(c, n) + Q_PART)
                low_of(0, 0).then_inc(input_step[c], 1)
                dve.wait_ge(even_high_ready[c], 2 * lone(c, n) + D_PART)
                low_of(1, 0).then_inc(input_step[c], 1)

            def row_alone(c, images, n):
                dve.wait_ge(input_step[c], at_step(c, n, "d_even_low"))
                dve.wait_ge(shared_ready[c], n)
                finish_parity(c, images, n, 1)
                dve.wait_ge(norm_ready[c], n + 1)
                input_alone(c, images, (c, n), n + 1, True)

            for k in range(2):
                nc.vector.memset(bn[:, :, OLD_AT + 3 * k:OLD_AT + 3 * k + 1], float(CHUNK * W))
            dve.wait_ge(pads_cleared, 1)
            for k in range(2):
                for b in range(FIRST.start, FIRST.stop):
                    dve.wait_ge(first_loaded["young"][k][b], 16)
                    if k == 1 and b == FIRST.stop - 1:
                        mean_of_sums(1)
                        square_of_sums(1)
                        variance_of_sums(1)
                    for half in range(2):
                        last = bn_half(k, k, b, half)
            last.then_inc(bn_taken, 1)
            dve.wait_ge(bn_taken, 1)
            channel_stats(1)
            group_variance(1)
            variance_eps(1)
            inverse_root(1)
            its_square(1)
            times_variance(1)
            scale_and_shift(1)
            dve.wait_ge(norm_ready["young"], 1)
            input_alone("young", FIRST, None, 1)

            def period(i, young, old, ahead):
                for k in range(2):
                    p = 2 * i + k
                    ny, no = HALF * i + CHUNK * k + 1, HALF * (i - 1) + CHUNK * k + 1

                    def step(r, stats=False, last_stats=False):
                        b = r - STATS_ROWS[0]

                        def bn_of(half):
                            if half == 0:
                                dve.wait_ge(chunk_loaded["young"][k], 16 * (i + 1))
                            bn_half((p + 2) % YOUNG_SLOTS, k, b, half)

                        g = i + 2
                        if not (young and old):
                            c, images, n = ("young", young, ny + r) if young else ("old", old, no + r)
                            row_alone(c, images, n)
                            if last_stats:
                                mean_of_sums(g)
                                square_of_sums(g)
                                variance_of_sums(g)
                                channel_stats(g)
                                group_variance(g)
                                variance_eps(g)
                                inverse_root(g)
                                its_square(g)
                                times_variance(g)
                                scale_and_shift(g)
                            final(c, images, chunk_of(c, p), r, n)
                            if stats:
                                bn_of(0)
                                bn_of(1)
                            return

                        n = ny + r
                        before = ("old", old, no + r)
                        finish_y("young", young, n)
                        low_of_earlier(before)
                        input_row("young", young, ("young", n), n + 1, before)
                        if stats:
                            bn_of(0)
                        input_differences("young", young, n + 1, before)
                        if last_stats:
                            mean_of_sums(g)
                        final("young", young, chunk_of("young", p), r, n)
                        if last_stats:
                            square_of_sums(g)
                        low_part("young", young, n + 1, 0, Q_PART)
                        if last_stats:
                            variance_of_sums(g)
                            channel_stats(g)

                        n = no + r
                        before = ("young", young, ny + r + 1)
                        finish_y("old", old, n)
                        if last_stats:
                            group_variance(g)
                        low_of_earlier(before)
                        if last_stats:
                            variance_eps(g)
                        input_row("old", old, ("old", n), n + 1, before)
                        if stats:
                            bn_of(1)
                        if last_stats:
                            inverse_root(g)
                        input_differences("old", old, n + 1, before)
                        if last_stats:
                            its_square(g)
                            times_variance(g)
                            scale_and_shift(g)
                        final("old", old, chunk_of("old", p), r, n)
                        low_part("old", old, n + 1, 0, Q_PART)

                    if ahead:
                        with dve.Fori(0, STATS_ROWS[0]) as r:
                            step(r)
                        with dve.Fori(*STATS_ROWS) as r:
                            step(r, True)
                        step(CHUNK - 2, False, k == 1)
                    else:
                        with dve.Fori(0, CHUNK - 1) as r:
                            step(r)

                    r = CHUNK - 1
                    if k == 0:
                        step(r)
                        continue
                    ny, no = ny + r, no + r
                    owed = ("old", old, no) if old else None
                    if young:
                        finish_y("young", young, ny)
                        low_of_earlier(owed)
                        dve.wait_ge(y_ready["young"], 2 * ny)
                        final("young", young, chunk_of("young", p), r, ny)
                        if not old:
                            dve.wait_ge(input_step["young"], at_step("young", ny, "d_even_low"))
                        if ahead:
                            input_row("young", ALL, None, ny + 1, None)
                            input_differences("young", ALL, ny + 1, None)
                            low_part("young", ALL, ny + 1, 0, Q_PART)
                            owed = ("young", ALL, ny + 1)
                    if old:
                        finish_y("old", old, no)
                        dve.wait_ge(y_ready["old"], 2 * no)
                        final("old", old, chunk_of("old", p), r, no)
                    if young:
                        carry = ("young", ny)
                        if ahead:
                            low_of_earlier(owed)
                            input_row("old", young, carry, no + 1, owed)
                            input_differences("old", young, no + 1, owed)
                            low_part("old", young, no + 1, 0, Q_PART)
                        else:
                            dve.wait_ge(low_ready["old"], 2 * no + D_PART)
                            dve.wait_ge(norm_ready["old"], no + 1)
                            input_alone("old", young, carry, no + 1)

            period(0, FIRST, None, True)
            period(1, ALL, FIRST, True)
            with dve.Fori(2, GROUPS - 1) as i:
                period(i, ALL, ALL, True)
            period(GROUPS - 1, ALL, ALL, False)
            period(GROUPS, None, ALL, False)


def kernel(x, L0_conv_kernel, L0_conv_bias):
    import numpy as np
    import concourse.bacc as bacc
    from concourse import mybir
    from concourse.bass_utils import run_bass_kernel_spmd

    nc = bacc.Bacc("TRN2", target_bir_lowering=False, num_devices=1)
    arrays, args = {}, []
    for name, a in (("x", x), ("taps", L0_conv_kernel), ("bias", L0_conv_bias)):
        a = np.ascontiguousarray(a)
        arrays[f"in_{name}"] = a
        args.append(nc.dram_tensor(f"in_{name}", a.shape, mybir.dt.from_np(a.dtype), kind="ExternalInput").ap())
    out = nc.dram_tensor("out", arrays["in_x"].shape, mybir.dt.float32, kind="ExternalOutput").ap()
    conv_scan_kernel(nc, *args, out)
    r = run_bass_kernel_spmd(nc, [arrays], core_ids=[0])
    return r.results[0]["out"]
```
